# Optimizing a Trainium2 kernel written in Bass

```python
import numpy as np
import jax
import jax.numpy as jnp

def _softmax(x, axis=-1):
    return jax.nn.softmax(x, axis=axis)
def _gelu(x):
    return jax.nn.gelu(x, approximate=True)
def _silu(x):
    return jax.nn.silu(x)
def _sigmoid(x):
    return jax.nn.sigmoid(x)
def _layernorm(x, axis=-1, eps=1e-5):
    m = jnp.mean(x, axis=axis, keepdims=True)
    v = jnp.var(x, axis=axis, keepdims=True)
    return (x - m) / jnp.sqrt(v + eps)
def _scatter_add(tgt, idx, src, axis=0):
    return tgt.at[idx].add(src)
def _segment_sum(src, seg, n):
    return jax.ops.segment_sum(src, seg, n)

kernel_name = 'mk_conv_seq_d1_conv_nhwc512_08b3f2'

def setup_inputs(seed: int = 0):
    np.random.seed(seed)
    _w = jnp.asarray
    def _rec_inputs():
        import jax
        import jax.numpy as jnp
        _gk = jax.random.key(seed)
        x = 7.22e-05 + 1 * jax.random.normal(jax.random.fold_in(_gk, 1), (16, 32, 32, 512), jnp.float32)
        return x
    x = _rec_inputs()
    def _L0_conv_setup():
        import jax, jax.numpy as jnp
        import numpy as np
        CH = 512
        HEADS = 8
        HEAD_CH = 64
        HIDDEN = HEADS * HEAD_CH
        GROUPS = 32
        EPS = 1e-05

        def group_norm(x, scale, offset):
            b, h, w, c = x.shape
            xg = x.reshape(b, h, w, GROUPS, c // GROUPS)
            mean = jnp.mean(xg, axis=(1, 2, 4), keepdims=True)
            var = jnp.var(xg, axis=(1, 2, 4), keepdims=True)
            xg = (xg - mean) * jax.lax.rsqrt(var + EPS)
            return xg.reshape(b, h, w, c) * scale + offset
        key = jax.random.key(seed)
        ks = jax.random.split(key, 6)
        x = jax.random.normal(ks[0], (16, 32, 32, CH), dtype=jnp.float32)
        gn_scale = jnp.ones((CH,), dtype=jnp.float32)
        gn_offset = jnp.zeros((CH,), dtype=jnp.float32)
        w_qkv = jax.random.normal(ks[1], (CH, 3 * HIDDEN), dtype=jnp.float32) * 0.02
        w_out = jax.random.normal(ks[2], (HIDDEN, CH), dtype=jnp.float32) * 0.02
        b_out = jax.random.normal(ks[3], (CH,), dtype=jnp.float32) * 0.02
        return {'x': x, 'gn_scale': gn_scale, 'gn_offset': gn_offset, 'w_qkv': w_qkv, 'w_out': w_out, 'b_out': b_out}
    _L0_conv_all = _L0_conv_setup()
    _L0_conv_in = {k: v for k, v in _L0_conv_all.items() if k in ('gn_scale', 'gn_offset', 'w_qkv', 'w_out', 'b_out', )}
    del _L0_conv_all

    return {
        "x": x,
        "L0_conv_gn_scale": _L0_conv_in["gn_scale"],
        "L0_conv_gn_offset": _L0_conv_in["gn_offset"],
        "L0_conv_w_qkv": _L0_conv_in["w_qkv"],
        "L0_conv_w_out": _L0_conv_in["w_out"],
        "L0_conv_b_out": _L0_conv_in["b_out"],
    }

def reference(x, L0_conv_gn_scale, L0_conv_gn_offset, L0_conv_w_qkv, L0_conv_w_out, L0_conv_b_out):
    import jax
    import jax.numpy as jnp
    def _L0_conv_ref(x, gn_scale, gn_offset, w_qkv, w_out, b_out):
        import jax, jax.numpy as jnp
        import numpy as np
        CH = 512
        HEADS = 8
        HEAD_CH = 64
        HIDDEN = HEADS * HEAD_CH
        GROUPS = 32
        EPS = 1e-05

        def group_norm(x, scale, offset):
            b, h, w, c = x.shape
            xg = x.reshape(b, h, w, GROUPS, c // GROUPS)
            mean = jnp.mean(xg, axis=(1, 2, 4), keepdims=True)
            var = jnp.var(xg, axis=(1, 2, 4), keepdims=True)
            xg = (xg - mean) * jax.lax.rsqrt(var + EPS)
            return xg.reshape(b, h, w, c) * scale + offset
        b, h, w, c = x.shape
        n = h * w
        xn = jax.nn.silu(group_norm(x, gn_scale, gn_offset))
        qkv = jnp.einsum('bxyc,cd->bxyd', xn, w_qkv)
        q, k, v = jnp.split(qkv, 3, axis=-1)

        def to_heads(a):
            a = a.reshape(b, n, HEADS, HEAD_CH)
            return jnp.transpose(a, (0, 2, 3, 1))
        q, k, v = (to_heads(q), to_heads(k), to_heads(v))
        q = q * HEAD_CH ** (-0.5)
        sim = jnp.einsum('bhdi,bhdj->bhij', q, k)
        attn = jax.nn.softmax(sim, axis=-1)
        out = jnp.einsum('bhij,bhdj->bhid', attn, v)
        out = jnp.transpose(out, (0, 2, 1, 3)).reshape(b, (h_ := h), w, HIDDEN) if False else jnp.transpose(out, (0, 2, 1, 3)).reshape(b, h, w, HIDDEN)
        out = jnp.einsum('bxyd,dc->bxyc', out, w_out) + b_out
        return out + x

    def _gn(v, G=32, eps=1e-5):
        B_, H_, W_, C_ = v.shape
        g = v.reshape(B_, H_, W_, G, C_ // G)
        m = jnp.mean(g, axis=(1, 2, 4), keepdims=True)
        s = jnp.var(g, axis=(1, 2, 4), keepdims=True)
        return ((g - m) / jnp.sqrt(s + eps)).reshape(v.shape)

    def _ln_c(v, eps=1e-6):
        m = jnp.mean(v, axis=-1, keepdims=True)
        s = jnp.var(v, axis=-1, keepdims=True)
        return (v - m) / jnp.sqrt(s + eps)

    def _ln_t(v, eps=1e-5):
        m = jnp.mean(v, axis=-1, keepdims=True)
        s = jnp.var(v, axis=-1, keepdims=True)
        return (v - m) / jnp.sqrt(s + eps)

    def _to_tokens(v):
        B_, H_, W_, C_ = v.shape
        return v.reshape(B_, H_ * W_, C_)
    def _from_tokens(t, like):
        return t.reshape(like.shape)

    x = _L0_conv_ref(x, L0_conv_gn_scale, L0_conv_gn_offset, L0_conv_w_qkv, L0_conv_w_out, L0_conv_b_out)
    return x


_drawn_inputs = setup_inputs


def setup_inputs(seed=0):
    import zlib

    import numpy as np

    out = dict(_drawn_inputs(seed))
    spreads = {'L0_conv_gn_scale': (1.0, 0.6), 'L0_conv_gn_offset': (0.0, 0.742)}
    factors = {'L0_conv_b_out': 3.014}
    for name, (base, spread) in spreads.items():
        noise = np.random.default_rng([zlib.crc32(name.encode()), seed]).standard_normal(out[name].shape)
        drawn = base * np.exp(spread * noise) if base else spread * noise
        out[name] = jnp.asarray(drawn.astype(out[name].dtype))
    for name, factor in factors.items():
        out[name] = (out[name] * factor).astype(out[name].dtype)
    return out
```

```python
import numpy as np
import concourse.bass as bass
from concourse import mybir
from contextlib import ExitStack

F32, F16, I32 = mybir.dt.float32, mybir.dt.float16, mybir.dt.int32
ACT = mybir.ActivationFunctionType
ALU = mybir.AluOpType
AX = mybir.AxisListType

P = 128
B, TOK, CH = 16, 1024, 512
HEADS, HD = 8, 64
GROUP = 16
EPS = 1e-5
CC = CH // P
TB = TOK // P
HALF = 512
VW = 130
LO = HD + 1
UNITS = 64
TOP = 2.0 ** 14
ROWC = 2.0 ** 15
SHIFT_UP = 8 * float(np.log(2.0))
EXPONENT = 0x7F800000
RSQRT_GUESS = float(0x5F3759DF)
NEWTON = 3
NORMED_MAX = float(GROUP * TOK) ** 0.5
Q_SCALE, K_SCALE, V_SCALE = 3, 4, 5
DVE_STEPS = 7
MAX_PER_W = [3, 3, 3, 3, 2, 2, 0, 0]


def head_slot(pair, hh):
    return (pair % 2) * 2 + hh


def rows_of(hh):
    return slice(hh * HD, hh * HD + HD)


def v_slot(head):
    return head + 2 if head < 6 else head - 6


def side_uses(step, u, first=False, last=False):
    uses = []
    w, hh = u % 8, u // 8
    nxt = (step, 1) if hh == 0 else ((step + 1) % 4, 0)
    if not (last and step == 3 and hh == 1):
        done = sum(MAX_PER_W[:w])
        for i in range(done, done + MAX_PER_W[w]):
            uses.append(("max", *nxt, i // 2, i % 2))
        if w == 6:
            uses += [("shift", *nxt, 0), ("shift", *nxt, 1)]
    if hh == 0 and w % 2 == 0 and not (last and step == 3):
        uses.append(("qk", (step + 1) % 4, "qk"[w // 2 % 2], w // 4))
    if u == 3 and not (first and step == 0):
        uses += [("ot", (step - 1) % 4, 0), ("ot", (step - 1) % 4, 1)]
    if step == 0 and u >= 8 and not first:
        uses.append(("out", u - 8))
    if step == 1 and u >= 8 and not last:
        uses.append(("xt", u - 8))
    if step == 2 and u in (5, 6) and not last:
        uses.append(("mean",) if u == 5 else ("var",))
    if step == 3 and u >= 8 and not last:
        uses.append(("v", u - 8))
    return uses


def image_of(use, b, step):
    if use[0] in ("xt", "mean", "var", "v") or (use[0] == "qk" and step == 3):
        return b + 1
    if use[0] == "out" or (use[0] == "ot" and step == 0):
        return b - 1
    return b


PROLOGUE = ([("xt", t) for t in range(TB)] + [("mean",), ("var",)]
            + [("qk", 0, "qk"[i % 2], i // 2) for i in range(4)] + [("v", t) for t in range(TB)]
            + [("max", 0, 0, i // 2, i % 2) for i in range(16)] + [("shift", 0, 0, 0), ("shift", 0, 0, 1)])
EPILOGUE = [("ot", 3, 0), ("ot", 3, 1)] + [("out", t) for t in range(TB)]
IMAGE_USES = [x for s in range(4) for u in range(16) for x in side_uses(s, u)]
WITH_HI = ("qk", "v", "ot")


class Count:
    PER_IMAGE = {"use": len(IMAGE_USES), "hi": sum(x[0] in WITH_HI for x in IMAGE_USES)}

    def __init__(self, use=0, hi=0, heads=0, marks=None, bank=0):
        self.use, self.hi, self.heads, self.bank = use, hi, heads, bank
        self.mark = dict(marks or {"qk": 0, "shift": 0, "v": 0, "ot": 0})

    def passed(self, use):
        self.use = self.use + 1
        self.bank = 1 - self.bank
        if use[0] in WITH_HI:
            self.hi = self.hi + 1
        if use[0] in self.mark:
            self.mark[use[0]] = self.use
        if use[0] == "shift" and use[3] == 1:
            self.heads = self.heads + 1

    def later(self, images):
        n = images * self.PER_IMAGE["use"]
        return Count(self.use + n, self.hi + images * self.PER_IMAGE["hi"], self.heads + images * HEADS,
                     {kind: at + n for kind, at in self.mark.items()}, self.bank)


def wait(eng, sem, count):
    if not isinstance(count, int) or count > 0:
        eng.wait_ge(sem, count)


def conv_attention(nc, x, gamma, beta, w_qkv, w_out, b_out, out):
    x_blocks = x.rearrange("b h w c -> (b h w) c").rearrange("(n p) c -> n p c", p=P)
    out_blocks = out.rearrange("b h w c -> (b h w) c").rearrange("(n p) c -> n p c", p=P)

    ctx = ExitStack()
    with ctx:
        def sb(name, shape, dt):
            return ctx.enter_context(nc.sbuf_tensor(name, shape, dt))

        def ps(name, shape, dt):
            return ctx.enter_context(nc.psum_tensor(name, shape, dt))

        def sem(name):
            return ctx.enter_context(nc.semaphore(name))

        ident32 = sb("ident32", [P, P], F32)
        ident16 = sb("ident16", [P, P], F16)
        group_mean = sb("group_mean", [P, P], F32)
        gam = sb("gam", [P, CC], F32)
        bet = sb("bet", [P, CC], F32)
        bias = sb("bias", [P, CH], F32)
        wq = sb("wq", [P, 2, CC, 3 * CH], F16)
        wo = sb("wo", [P, 2, CC, CH], F16)
        red = sb("red", [P, 8], F32)
        top = sb("top", [P, 8], F32)
        pw = sb("pw", [P, 8], F32)
        sc = sb("sc", [P, 8], F32)
        inv = sb("inv", [P, 8], F32)
        tot = sb("tot", [P, 8], F32)
        cns = sb("cns", [P, 4], F32)
        absg = sb("absg", [P, CC], F32)
        absb = sb("absb", [P, CC], F32)
        bound = sb("bound", [P, CC], F32)
        bound16 = sb("bound16", [P, CC], F16)
        x_in = sb("x_in", [P, 2, CH], F32)
        work = sb("work", [P, 6 * TOK], F32)
        xT = work[:, 0:4 * TOK].rearrange("p (c n) -> p c n", c=CC)
        z = work[:, 4 * TOK:5 * TOK]
        th = work[:, 5 * TOK:6 * TOK]
        st = sb("st", [P, CC, 12], F32)
        mv = sb("mv", [P, CC, 2], F32)
        gn = sb("gn", [P, 16, CC], F32)
        gmean, dev, dev2, vd, veps, half_v, three_halves, half_bits, root, a_c, ma_c, b_c, ah, bh, az, bz = (
            gn[:, i, :] for i in range(16))
        nt = sb("nt", [P, 2, CC], F32)
        xn = sb("xn", [P, 2, CC, TOK], F16)
        K1 = sb("K1", [P, 4, TOK], F16)
        K2 = sb("K2", [P, 4, TOK], F16)
        Q1 = sb("Q1", [P, 4, TOK], F16)
        Q2 = sb("Q2", [P, 4, TOK], F16)
        V = sb("V", [P, TB, 10, VW], F16)
        mx = sb("mx", [P, 2, TB, 2], F32)
        mx8 = sb("mx8", [P, TB], F32)
        ms = sb("ms", [P, 2, TB], F16)
        P32 = sb("P32", [P, 2, 2 * HALF], F32)
        Ph = sb("Ph", [P, 4, 2 * HALF], F16)
        Pl = sb("Pl", [P, 4, 2 * HALF], F16)
        pv_lo = sb("pv_lo", [P, 2, 4, HD], F32)
        pv_sum = sb("pv_sum", [P, 2, 4, HD], F32)
        den = sb("den", [P, 2, 4], F32)
        O32 = sb("O32", [P, 2, TB, P], F32)
        OT = sb("OT", [P, 2, CC, TOK], F16)
        res = sb("res", [P, 4, CH], F32)

        w_stage = work[:, :].rearrange("p (c n) -> p c n", c=CC)
        wo_stage = P32[:, :, :].rearrange("p a b -> p (a b)").rearrange("p (c n) -> p c n", c=CC)
        w_abs = xn[:, :, :, :].rearrange("p a c n -> p (a c n)")[:, 0:CC * 3 * CH].rearrange(
            "p (c n) -> p c n", c=CC)

        ST = ps("ST", [P, 2, 2 * HALF], F32)
        PV = ps("PV", [P, 2, 512], F32)
        SD = ps("SD", [P, 2, 512], F32)

        bound_psum = ST[:, :, :].rearrange("p a (b n) -> p (a b) n", n=512)
        pv_blocks = PV[:, :, 0:2 * (LO + HD)].rearrange("p a (q c) -> p a q c", q=2)

        w_loaded = sem("w_loaded")
        const_ready = sem("const_ready")
        maxima_in = sem("maxima_in")
        maxima_out = sem("maxima_out")
        setup_step = sem("setup_step")
        bound_in = sem("bound_in")
        bound_out = sem("bound_out")
        setup_done = sem("setup_done")
        x_loaded = [sem(f"x_loaded{i}") for i in range(2)]
        res_loaded = [sem(f"res_loaded{i}") for i in range(4)]
        res_biased = sem("res_biased")
        stored = [sem(f"stored{i}") for i in range(4)]
        side_filled = sem("side_filled")
        side_hi = sem("side_hi")
        side_drained = sem("side_drained")
        bn_done = sem("bn_done")
        chan_stats = sem("chan_stats")
        dve_step = sem("dve_step")
        dev_ready = sem("dev_ready")
        guess_ready = sem("guess_ready")
        newton_step = sem("newton_step")
        coef_ready = sem("coef_ready")
        silu_ready = sem("silu_ready")
        xn_f32 = sem("xn_f32")
        xn_hi = sem("xn_hi")
        xn_lo = sem("xn_lo")
        v_moved = sem("v_moved")
        mx8_ready = sem("mx8_ready")
        shift_ready = sem("shift_ready")
        scores_ready = sem("scores_ready")
        exp_done = sem("exp_done")
        lo_dve = sem("lo_dve")
        lo_pool = sem("lo_pool")
        pv_done = sem("pv_done")
        pv_lo_out = sem("pv_lo_out")
        pv_out = sem("pv_out")
        o_normed = sem("o_normed")

        block = ctx.enter_context(nc.Block())

        @block.sync
        def _(sp):
            sp.dma_start(w_stage, w_qkv.rearrange("(c p) n -> p c n", p=P)).then_inc(w_loaded, 16)
            sp.dma_start(wo_stage, w_out.rearrange("(c p) n -> p c n", p=P)).then_inc(w_loaded, 16)
            sp.dma_start(gam[:], gamma.rearrange("(c p) -> p c", p=P), allow_slow_non_contiguous=True).then_inc(w_loaded, 16)
            sp.dma_start(bet[:], beta.rearrange("(c p) -> p c", p=P), allow_slow_non_contiguous=True).then_inc(w_loaded, 16)
            sp.dma_start(bias[:], b_out.rearrange("(o c) -> o c", o=1).to_broadcast([P, CH])
                         ).then_inc(w_loaded, 16)

            def load_x(image, t, filled):
                src = x_blocks[bass.ds(sp.snap(image * TB + t), 1)].rearrange("o p c -> p (o c)")
                wait(sp, side_filled, filled)
                sp.dma_start(x_in[:, t % 2, :], src).then_inc(x_loaded[t % 2], 16)

            def load_res(image, t):
                src = x_blocks[bass.ds(sp.snap(image * TB + t), 1)].rearrange("o p c -> p (o c)")
                wait(sp, stored[t % 4], 32 * image + 16 * (t // 4))
                sp.dma_start(res[:, t % 4, :], src).then_inc(res_loaded[t % 4], 16)

            def store(image, t, drained):
                dst = out_blocks[bass.ds(sp.snap(image * TB + t), 1)].rearrange("o p c -> p (o c)")
                wait(sp, side_drained, drained)
                sp.dma_start(dst, res[:, t % 4, :]).then_inc(stored[t % 4], 16)

            def step(b, s, cnt, first=False, last=False):
                filled = [cnt.use, cnt.use]
                if s == 1:
                    for t in range(4):
                        load_res(b, t)
                for u in range(16):
                    for use in side_uses(s, u, first, last):
                        cnt.passed(use)
                        if use[0] == "xt":
                            load_x(b + 1, use[1], filled[use[1]])
                            filled.append(cnt.use)
                        if use[0] == "out":
                            store(b - 1, use[1], cnt.use)
                            if use[1] < 4:
                                load_res(b - 1, use[1] + 4)

            cnt = Count()
            for use in PROLOGUE:
                cnt.passed(use)
                if use[0] == "xt":
                    load_x(0, use[1], cnt.use - 2)
            step(0, 0, cnt, first=True)
            with sp.Fori(0, B - 1) as b:
                now = cnt.later(b)
                for s in (1, 2, 3):
                    step(b, s, now)
                step(b + 1, 0, now)
            now = cnt.later(B - 1)
            for s in (1, 2, 3):
                step(B - 1, s, now, last=True)
            for use in EPILOGUE:
                now.passed(use)
                if use[0] == "out":
                    store(B - 1, use[1], now.use)
                    if use[1] < 4:
                        load_res(B - 1, use[1] + 4)
            for t in range(4):
                sp.wait_ge(stored[t], 32 * B)

        @block.gpsimd
        def _(pool):
            nc.gpsimd.memset(ident32[:], 0.0).then_inc(const_ready, 1)
            nc.gpsimd.memset(group_mean[:], 1.0 / GROUP).then_inc(const_ready, 1)
            pool.wait_ge(const_ready, 2)
            nc.gpsimd.affine_select(out=ident32[:], in_=ident32[:], compare_op=ALU.not_equal, fill=1.0, base=0,
                                    pattern=[[-1, P]], channel_multiplier=1).then_inc(const_ready, 1)
            grouped = group_mean[:].rearrange("p (g c) -> p g c", c=GROUP)
            nc.gpsimd.affine_select(out=grouped, in_=grouped, compare_op=ALU.is_ge, fill=0.0, base=0,
                                    pattern=[[-GROUP, P // GROUP], [0, GROUP]], channel_multiplier=1
                                    ).then_inc(const_ready, 1)
            pool.wait_ge(const_ready, 4)
            nc.gpsimd.affine_select(out=grouped, in_=grouped, compare_op=ALU.is_ge, fill=0.0, base=GROUP - 1,
                                    pattern=[[GROUP, P // GROUP], [0, GROUP]], channel_multiplier=-1
                                    ).then_inc(const_ready, 1)
            pool.wait_ge(maxima_in, 1)
            nc.gpsimd.partition_all_reduce(top[:, 0:3], red[:, 0:3], P, bass.bass_isa.ReduceOp.max
                                           ).then_inc(maxima_out, 1)
            pool.wait_ge(setup_done, 1)

            def newton(image):
                n = 4 * NEWTON * image
                pool.wait_ge(guess_ready, image + 1)
                for i in range(0, 4 * NEWTON, 4):
                    nc.gpsimd.tensor_tensor(nt[:, 0, :], root, root, ALU.mult).then_inc(newton_step, 1)
                    pool.wait_ge(newton_step, n + i + 1)
                    nc.gpsimd.tensor_tensor(nt[:, 1, :], nt[:, 0, :], half_v, ALU.mult).then_inc(newton_step, 1)
                    pool.wait_ge(newton_step, n + i + 2)
                    nc.gpsimd.tensor_tensor(nt[:, 0, :], three_halves, nt[:, 1, :], ALU.subtract
                                            ).then_inc(newton_step, 1)
                    pool.wait_ge(newton_step, n + i + 3)
                    nc.gpsimd.tensor_tensor(root, root, nt[:, 0, :], ALU.mult).then_inc(newton_step, 1)
                    pool.wait_ge(newton_step, n + i + 4)

            def low_xn(image, c):
                pool.wait_ge(xn_hi, 4 * image + c + 1)
                nc.gpsimd.tensor_tensor(xn[:, 1, c, :], xT[:, c, :], xn[:, 0, c, :], ALU.subtract
                                        ).then_inc(xn_lo, 1)

            def add_bias(image, t):
                pool.wait_ge(res_loaded[t % 4], 32 * image + 16 * (t // 4) + 16)
                nc.gpsimd.tensor_tensor(res[:, t % 4, :], res[:, t % 4, :], bias[:], ALU.add
                                        ).then_inc(res_biased, 1)

            def low_probs(b, v):
                pool.wait_ge(exp_done, UNITS * b + v + 1)
                wait(pool, pv_done, UNITS * b + v - 3)
                nc.gpsimd.tensor_tensor(Pl[:, v % 4, :], P32[:, v % 2, :], Ph[:, v % 4, :], ALU.subtract
                                        ).then_inc(lo_pool, 1)

            def normalise(b, half):
                pool.wait_ge(pv_out, 16 * b + half + 1)
                pair, hh, q = half // 4 % 4, half // 2 % 2, half % 2
                nc.gpsimd.tensor_tensor(O32[:, pair % 2, 4 * q:4 * q + 4, rows_of(hh)], pv_sum[:, half % 2],
                                        den[:, half % 2, :].unsqueeze(2).to_broadcast([P, 4, HD]), ALU.mult
                                        ).then_inc(o_normed, 1)

            def step(b, s, first=False, last=False):
                for u in range(16):
                    v = 16 * s + u
                    if v % 2 == 0 and not (first and v == 0):
                        low_probs(b, v - 1)
                    if v % 4 == 1 and not (first and v == 1):
                        normalise(b, v // 4 - 1)
                    if s == 2 and u == 6 and not last:
                        newton(b + 1)
                    if s == 2 and 9 <= u < 13 and not last:
                        low_xn(b + 1, u - 9)
                    if s == 2 and u >= 12:
                        add_bias(b, u - 12)
                    if s == 0 and 11 <= u < 15 and not first:
                        add_bias(b - 1, u - 7)

            newton(0)
            for c in range(CC):
                low_xn(0, c)
            step(0, 0, first=True)
            with pool.Fori(0, B - 1) as b:
                for s in (1, 2, 3):
                    step(b, s)
                step(b + 1, 0)
            for s in (1, 2, 3):
                step(B - 1, s, last=True)
            low_probs(B - 1, UNITS - 1)
            normalise(B - 1, 15)
            for t in range(4, 8):
                add_bias(B - 1, t)

        @block.scalar
        def _(act):
            act.wait_ge(setup_done, 1)

            def side(use, image, cnt):
                bank = cnt.bank
                if use[0] in WITH_HI:
                    act.wait_ge(side_filled, cnt.use + 1)
                if use[0] == "qk":
                    _, pair, which, half = use
                    dst, col = (Q1, Q_SCALE) if which == "q" else (K1, K_SCALE)
                    for hh in range(2):
                        r = rows_of(hh)
                        hi = nc.scalar.activation(dst[r, head_slot(pair, hh), bass.ts(half, HALF)],
                                                  SD[r, bank, :], ACT.Identity, scale=sc[r, col:col + 1])
                    hi.then_inc(side_hi, 1)
                if use[0] == "v":
                    wait(act, v_moved, image)
                    nc.scalar.activation(V[:, use[1], 2:10, 0:HD],
                                         SD[:, bank, :].rearrange("p (h d) -> p h d", d=HD), ACT.Identity,
                                         scale=sc[:, V_SCALE:V_SCALE + 1]).then_inc(side_hi, 1)
                if use[0] == "ot":
                    _, pair, half = use
                    nc.scalar.activation(OT[:, 0, pair, bass.ts(half, HALF)], SD[:, bank, :], ACT.Copy
                                         ).then_inc(side_hi, 1)
                cnt.passed(use)

            def silu_parts(image, c):
                act.wait_ge(coef_ready, image + 1)
                wait(act, xn_f32, 4 * image + c)
                nc.scalar.activation(z, xT[:, c, :], ACT.Identity, scale=az[:, c:c + 1], bias=bz[:, c:c + 1])
                nc.scalar.activation(th, xT[:, c, :], ACT.Tanh, scale=ah[:, c:c + 1], bias=bh[:, c:c + 1]
                                     ).then_inc(silu_ready, 1)

            def exponentials(b, v):
                act.wait_ge(scores_ready, UNITS * b + v + 1)
                if v % 2 == 0:
                    wait(act, lo_dve, 32 * b + v // 2)
                else:
                    wait(act, lo_pool, 32 * b + v // 2)
                nc.scalar.activation(P32[:, v % 2, :], ST[:, v % 2, :], ACT.Exp, scale=cns[:, 0:1])
                wait(act, pv_done, UNITS * b + v - 3)
                nc.scalar.activation(Ph[:, v % 4, :], ST[:, v % 2, :], ACT.Exp, scale=cns[:, 0:1]
                                     ).then_inc(exp_done, 1)

            def low_sums(b, half):
                act.wait_ge(pv_done, UNITS * b + 4 * half + 4)
                wait(act, pv_out, 16 * b + half - 1)
                nc.scalar.activation(pv_lo[:, half % 2].rearrange("p (a q) d -> p a q d", a=2),
                                     pv_blocks[:, :, :, LO:LO + HD], ACT.Copy).then_inc(pv_lo_out, 1)

            def step(b, s, cnt, first=False, last=False):
                for u in range(16):
                    v = 16 * s + u
                    exponentials(b, v)
                    if v % 4 == 1 and not (first and v == 1):
                        low_sums(b, v // 4 - 1)
                    for use in side_uses(s, u, first, last):
                        side(use, image_of(use, b, s), cnt)
                    if s == 2 and 8 <= u < 12 and not last:
                        silu_parts(b + 1, u - 8)

            cnt = Count()
            for use in PROLOGUE:
                side(use, 0, cnt)
                if use[0] == "var":
                    for c in range(CC):
                        silu_parts(0, c)
            step(0, 0, cnt, first=True)
            with act.Fori(0, B - 1) as b:
                now = cnt.later(b)
                for s in (1, 2, 3):
                    step(b, s, now)
                step(b + 1, 0, now)
            now = cnt.later(B - 1)
            for s in (1, 2, 3):
                step(B - 1, s, now, last=True)
            low_sums(B - 1, 15)
            for use in EPILOGUE:
                side(use, B - 1, now)

        @block.vector
        def _(dve):
            steps = [0]

            def then(ins):
                steps[0] += 1
                ins.then_inc(setup_step, 1)
                dve.wait_ge(setup_step, steps[0])

            def scale_of(dst, inverse, size):
                n = size.shape[1]
                then(nc.vector.tensor_scalar(size, size, 1e-30, None, ALU.max))
                then(nc.vector.tensor_scalar(pw[:, 0:n].bitcast(I32), size.bitcast(I32), EXPONENT, None,
                                             ALU.bitwise_and))
                then(nc.vector.tensor_scalar(inverse, pw[:, 0:n], 1.0 / TOP, None, ALU.mult))
                then(nc.vector.reciprocal(dst, inverse))

            nc.vector.memset(V[:], 1.0)
            nc.vector.memset(K2[:], ROWC)
            nc.vector.memset(three_halves, 1.5)
            dve.wait_ge(const_ready, 5)
            nc.vector.tensor_copy(ident16[:], ident32[:])
            dve.wait_ge(w_loaded, 16 * 5)
            then(nc.vector.tensor_reduce(red[:, 0:1], w_stage, AX.XY, ALU.max, apply_absolute_value=True))
            then(nc.vector.tensor_reduce(red[:, 1:2], wo_stage, AX.XY, ALU.max, apply_absolute_value=True))
            then(nc.vector.scalar_tensor_tensor(out=absg[:], in0=gam[:], scalar=-1.0, in1=gam[:],
                                                op0=ALU.mult, op1=ALU.max))
            then(nc.vector.scalar_tensor_tensor(out=absb[:], in0=bet[:], scalar=-1.0, in1=bet[:],
                                                op0=ALU.mult, op1=ALU.max))
            then(nc.vector.scalar_tensor_tensor(out=bound[:], in0=absg[:], scalar=NORMED_MAX, in1=absb[:],
                                                op0=ALU.mult, op1=ALU.add))
            nc.vector.tensor_reduce(red[:, 2:3], bound[:], AX.X, ALU.max).then_inc(maxima_in, 1)
            dve.wait_ge(maxima_out, 1)
            scale_of(sc[:, 0:3], inv[:, 0:3], top[:, 0:3])
            then(nc.vector.tensor_scalar(wq[:, 0], w_stage, sc[:, 0:1], None, ALU.mult))
            then(nc.vector.scalar_tensor_tensor(out=wq[:, 1], in0=w_stage, scalar=sc[:, 0:1], in1=wq[:, 0],
                                                op0=ALU.mult, op1=ALU.subtract))
            then(nc.vector.tensor_scalar(wo[:, 0], wo_stage, sc[:, 1:2], None, ALU.mult))
            then(nc.vector.scalar_tensor_tensor(out=wo[:, 1], in0=wo_stage, scalar=sc[:, 1:2], in1=wo[:, 0],
                                                op0=ALU.mult, op1=ALU.subtract))
            then(nc.vector.scalar_tensor_tensor(out=w_abs, in0=wq[:, 0], scalar=-1.0, in1=wq[:, 0],
                                                op0=ALU.mult, op1=ALU.max))
            nc.vector.tensor_scalar(bound16[:], bound[:], sc[:, 2:3], None, ALU.mult).then_inc(bound_in, 1)
            dve.wait_ge(bound_out, 1)
            for i in range(3):
                then(nc.vector.tensor_reduce(top[:, 3 + i:4 + i], bound_psum[:, i, :], AX.X, ALU.max))
            scale_of(sc[:, 3:6], inv[:, 3:6], top[:, 3:6])
            then(nc.vector.tensor_scalar(tot[:, 0:3], inv[:, 3:6], inv[:, 0:1], inv[:, 2:3], ALU.mult, ALU.mult))
            then(nc.vector.tensor_scalar(cns[:, 0:1], tot[:, 0:1], tot[:, 1:2], HD ** -0.5, ALU.mult, ALU.mult))
            then(nc.vector.tensor_scalar(cns[:, 1:2], tot[:, 2:3], inv[:, 1:2], None, ALU.mult))
            then(nc.vector.reciprocal(cns[:, 2:3], cns[:, 0:1]))
            nc.vector.tensor_scalar(cns[:, 3:4], cns[:, 2:3], SHIFT_UP, None, ALU.mult).then_inc(setup_done, 1)
            dve.wait_ge(setup_done, 1)

            def side(use, b, image, cnt):
                kind, bank = use[0], cnt.bank
                if kind == "shift" and use[3] == 0:
                    dve.wait_ge(side_drained, cnt.use)
                    nc.vector.tensor_reduce(mx8[:], mx[:, use[2]], AX.X, ALU.max).then_inc(mx8_ready, 1)
                    dve.wait_ge(mx8_ready, cnt.heads + 1)
                    nc.vector.tensor_scalar(ms[:, use[2], :], mx8[:], cns[:, 3:4], -1.0 / (HD * ROWC),
                                            ALU.subtract, ALU.mult).then_inc(shift_ready, 1)
                dve.wait_ge(side_filled, cnt.use + 1)
                if kind in WITH_HI:
                    dve.wait_ge(side_hi, cnt.hi + 1)
                if kind == "max":
                    _, pair, hh, qb, kh = use
                    nc.vector.reduce_max(mx[:, hh, qb, kh:kh + 1], SD[:, bank, :], AX.X).then_inc(side_drained, 1)
                if kind == "shift":
                    _, pair, hh, half = use
                    r = rows_of(1 - hh)
                    nc.vector.tensor_copy(Q2[r, head_slot(pair, hh), bass.ts(half, HALF)], SD[r, bank, :]
                                          ).then_inc(side_drained, 1)
                if kind == "qk":
                    _, pair, which, half = use
                    cols = bass.ts(half, HALF)
                    for hh in range(2):
                        r, other, slot = rows_of(hh), rows_of(1 - hh), head_slot(pair, hh)
                        if which == "q":
                            nc.vector.tensor_copy(Q1[other, slot, cols], Q1[r, slot, cols])
                            low = nc.vector.scalar_tensor_tensor(
                                out=Q2[r, slot, cols], in0=SD[r, bank, :], scalar=sc[r, Q_SCALE:Q_SCALE + 1],
                                in1=Q1[r, slot, cols], op0=ALU.mult, op1=ALU.subtract)
                        else:
                            nc.vector.tensor_copy(K2[r, slot, cols], K1[r, slot, cols])
                            low = nc.vector.scalar_tensor_tensor(
                                out=K1[other, slot, cols], in0=SD[r, bank, :], scalar=sc[r, K_SCALE:K_SCALE + 1],
                                in1=K1[r, slot, cols], op0=ALU.mult, op1=ALU.subtract)
                    low.then_inc(side_drained, 1)
                if kind == "v":
                    wait(dve, v_moved, image)
                    nc.vector.scalar_tensor_tensor(
                        out=V[:, use[1], 2:10, LO:LO + HD], in0=SD[:, bank, :].rearrange("p (h d) -> p h d", d=HD),
                        scalar=sc[:, V_SCALE:V_SCALE + 1], in1=V[:, use[1], 2:10, 0:HD],
                        op0=ALU.mult, op1=ALU.subtract).then_inc(side_drained, 1)
                if kind == "ot":
                    _, pair, half = use
                    cols = bass.ts(half, HALF)
                    nc.vector.tensor_tensor(OT[:, 1, pair, cols], SD[:, bank, :], OT[:, 0, pair, cols],
                                            ALU.subtract).then_inc(side_drained, 1)
                if kind == "out":
                    dve.wait_ge(res_biased, TB * image + use[1] + 1)
                    nc.vector.scalar_tensor_tensor(out=res[:, use[1] % 4, :], in0=SD[:, bank, :],
                                                   scalar=cns[:, 1:2], in1=res[:, use[1] % 4, :],
                                                   op0=ALU.mult, op1=ALU.add).then_inc(side_drained, 1)
                if kind == "xt":
                    wait(dve, xn_lo, CC * image)
                    wait(dve, xn_hi, CC * image)
                    nc.vector.tensor_copy(xT[:, :, bass.ts(use[1], P)],
                                          SD[:, bank, :].rearrange("p (c n) -> p c n", c=CC)
                                          ).then_inc(side_drained, 1)
                if kind == "mean":
                    n = DVE_STEPS * image
                    nc.vector.tensor_copy(gmean, SD[:, bank, 0:CC]).then_inc(side_drained, 1)
                    dve.wait_ge(side_drained, cnt.use + 1)
                    nc.vector.tensor_tensor(dev, mv[:, :, 0], gmean, ALU.subtract).then_inc(dve_step, 1)
                    dve.wait_ge(dve_step, n + 1)
                    nc.vector.tensor_tensor(dev2, dev, dev, ALU.mult).then_inc(dve_step, 1)
                    dve.wait_ge(dve_step, n + 2)
                    nc.vector.tensor_tensor(vd, dev2, mv[:, :, 1], ALU.add).then_inc(dev_ready, 1)
                if kind == "var":
                    n = DVE_STEPS * image + 2
                    nc.vector.tensor_scalar(veps, SD[:, bank, 0:CC], EPS, None, ALU.add
                                            ).then_inc(side_drained, 1)
                    dve.wait_ge(side_drained, cnt.use + 1)
                    nc.vector.tensor_scalar(half_v, veps, 0.5, None, ALU.mult)
                    nc.vector.tensor_scalar(half_bits.bitcast(I32), veps.bitcast(I32), 1, None,
                                            ALU.logical_shift_right).then_inc(dve_step, 1)
                    dve.wait_ge(dve_step, n + 1)
                    nc.vector.tensor_scalar(root.bitcast(I32), half_bits.bitcast(I32), -1.0, RSQRT_GUESS,
                                            ALU.mult, ALU.add).then_inc(guess_ready, 1)
                cnt.passed(use)

            def channel_stats(image, i, cnt):
                dve.wait_ge(side_drained, cnt.use)
                c, half = i // 2, i % 2
                stats = nc.vector.bn_stats(st[:, c, 6 * half:6 * half + 6], xT[:, c, bass.ts(half, HALF)])
                if i == 7:
                    stats.then_inc(bn_done, 1)

            def aggregate(image):
                for c in range(CC):
                    aggr = nc.vector.bn_aggr(mv[:, c, :], st[:, c, :])
                aggr.then_inc(chan_stats, 1)
                dve.wait_ge(chan_stats, image + 1)

            def coefficients(image):
                n = DVE_STEPS * image + 3
                dve.wait_ge(newton_step, 4 * NEWTON * (image + 1))
                nc.vector.tensor_tensor(a_c, gam[:], root, ALU.mult).then_inc(dve_step, 1)
                dve.wait_ge(dve_step, n + 1)
                nc.vector.tensor_tensor(ma_c, gmean, a_c, ALU.mult).then_inc(dve_step, 1)
                dve.wait_ge(dve_step, n + 2)
                nc.vector.tensor_tensor(b_c, bet[:], ma_c, ALU.subtract).then_inc(dve_step, 1)
                dve.wait_ge(dve_step, n + 3)
                nc.vector.tensor_scalar(ah, a_c, 0.5, None, ALU.mult)
                nc.vector.tensor_scalar(bh, b_c, 0.5, None, ALU.mult).then_inc(dve_step, 1)
                dve.wait_ge(dve_step, n + 4)
                nc.vector.tensor_scalar(az, ah, sc[:, 2:3], None, ALU.mult)
                nc.vector.tensor_scalar(bz, bh, sc[:, 2:3], None, ALU.mult).then_inc(coef_ready, 1)

            def silu(image, c):
                dve.wait_ge(silu_ready, CC * image + c + 1)
                nc.vector.scalar_tensor_tensor(out=xT[:, c, :], in0=th, scalar=1.0, in1=z,
                                               op0=ALU.add, op1=ALU.mult).then_inc(xn_f32, 1)
                dve.wait_ge(xn_f32, CC * image + c + 1)
                nc.vector.tensor_copy(xn[:, 0, c, :], xT[:, c, :]).then_inc(xn_hi, 1)

            def low_probs(b, v):
                dve.wait_ge(exp_done, UNITS * b + v + 1)
                wait(dve, pv_done, UNITS * b + v - 3)
                nc.vector.tensor_tensor(Pl[:, v % 4, :], P32[:, v % 2, :], Ph[:, v % 4, :], ALU.subtract
                                        ).then_inc(lo_dve, 1)

            def sums(b, half):
                dve.wait_ge(pv_lo_out, 16 * b + half + 1)
                wait(dve, o_normed, 16 * b + half - 1)
                nc.vector.reciprocal(den[:, half % 2, :].rearrange("p (a q) -> p a q", a=2),
                                     pv_blocks[:, :, :, HD])
                nc.vector.tensor_tensor(pv_sum[:, half % 2].rearrange("p (a q) d -> p a q d", a=2),
                                        pv_blocks[:, :, :, 0:HD],
                                        pv_lo[:, half % 2].rearrange("p (a q) d -> p a q d", a=2), ALU.add
                                        ).then_inc(pv_out, 1)

            def move_v(b, cnt):
                wait(dve, pv_done, UNITS * b)
                dve.wait_ge(side_drained, cnt.use)
                nc.vector.tensor_copy(V[:, :, 0:2, :], V[:, :, 8:10, :]).then_inc(v_moved, 1)

            def step(b, s, cnt, first=False, last=False):
                for u in range(16):
                    v = 16 * s + u
                    if v % 2 == 1:
                        low_probs(b, v - 1)
                    for use in side_uses(s, u, first, last):
                        side(use, b, image_of(use, b, s), cnt)
                    if v % 4 == 1 and not (first and v == 1):
                        sums(b, v // 4 - 1)
                    if s == 0 and u == 7:
                        move_v(b, cnt)
                    if s == 2 and not last:
                        if u < 4:
                            channel_stats(b + 1, 2 * u, cnt)
                            channel_stats(b + 1, 2 * u + 1, cnt)
                        if u == 4:
                            aggregate(b + 1)
                        if u == 7:
                            coefficients(b + 1)
                        if 9 <= u < 13:
                            silu(b + 1, u - 9)

            cnt = Count()
            for use in PROLOGUE:
                side(use, 0, 0, cnt)
                if use == ("xt", TB - 1):
                    for i in range(8):
                        channel_stats(0, i, cnt)
                    dve.wait_ge(bn_done, 1)
                    aggregate(0)
                if use[0] == "var":
                    coefficients(0)
                    for c in range(CC):
                        silu(0, c)
            step(0, 0, cnt, first=True)
            with dve.Fori(0, B - 1) as b:
                now = cnt.later(b)
                for s in (1, 2, 3):
                    step(b, s, now)
                step(b + 1, 0, now)
            now = cnt.later(B - 1)
            for s in (1, 2, 3):
                step(B - 1, s, now, last=True)
            sums(B - 1, 15)
            for use in EPILOGUE:
                side(use, B - 1, B - 1, now)

        @block.tensor
        def _(pe):
            pe.wait_ge(bound_in, 1)
            for i in range(3):
                for c in range(CC):
                    last_mm = nc.tensor.matmul(bound_psum[:, i, :], bound16[:, c:c + 1].to_broadcast([P, P]),
                                               w_abs[:, c, i * CH:(i + 1) * CH], start=(c == 0),
                                               stop=(c == CC - 1))
            last_mm.then_inc(bound_out, 1)
            pe.wait_ge(setup_done, 1)

            def three_passes(bank, stationary, moving):
                for c in range(CC):
                    for i, j in ((0, 0), (0, 1), (1, 0)):
                        ins = nc.tensor.matmul(SD[:, bank, :], stationary(i, c), moving(j, c),
                                               start=(c == 0 and i + j == 0), stop=(c == CC - 1 and i == 1))
                return ins

            def side(use, image, cnt):
                kind, bank = use[0], cnt.bank
                wait(pe, side_drained, cnt.use - 1)
                if kind == "max":
                    _, pair, hh, qb, kh = use
                    r, slot = rows_of(hh), head_slot(pair, hh)
                    if qb == kh == 0:
                        wait(pe, side_drained, cnt.mark["qk"])
                    ins = nc.tensor.matmul(SD[:, bank, :], Q1[r, slot, bass.ts(qb, P)],
                                           K1[r, slot, bass.ts(kh, HALF)], start=True, stop=True)
                if kind == "shift":
                    _, pair, hh, half = use
                    pe.wait_ge(shift_ready, cnt.heads + 1)
                    for i in range(4):
                        qb = 4 * half + i
                        ins = nc.tensor.matmul(SD[:, bank, bass.ts(i, P)],
                                               ms[:, hh, qb:qb + 1].to_broadcast([P, P]), ident16[:],
                                               start=True, stop=True)
                if kind == "qk":
                    _, pair, which, half = use
                    col = pair * P + (0 if which == "q" else CH)
                    pe.wait_ge(xn_lo, CC * (image + 1))
                    ins = three_passes(bank, lambda i, c: wq[:, i, c, col:col + P],
                                       lambda j, c: xn[:, j, c, bass.ts(half, HALF)])
                if kind == "v":
                    ins = three_passes(bank, lambda i, c: xn[:, i, c, bass.ts(use[1], P)],
                                       lambda j, c: wq[:, j, c, 2 * CH:3 * CH])
                if kind == "ot":
                    _, pair, half = use
                    pe.wait_ge(o_normed, 16 * image + 4 * (pair + 1))
                    for i in range(4):
                        ins = nc.tensor.transpose(SD[:, bank, bass.ts(i, P)], O32[:, pair % 2, 4 * half + i, :],
                                                  ident32[:])
                if kind == "out":
                    pe.wait_ge(side_drained, cnt.mark["ot"])
                    ins = three_passes(bank, lambda i, c: OT[:, i, c, bass.ts(use[1], P)],
                                       lambda j, c: wo[:, j, c, :])
                if kind == "xt":
                    t = use[1]
                    pe.wait_ge(x_loaded[t % 2], 16 * (TB // 2 * image + t // 2 + 1))
                    for c in range(CC):
                        ins = nc.tensor.transpose(SD[:, bank, bass.ts(c, P)], x_in[:, t % 2, bass.ts(c, P)],
                                                  ident32[:])
                if kind == "mean":
                    pe.wait_ge(chan_stats, image + 1)
                    ins = nc.tensor.matmul(SD[:, bank, 0:CC], group_mean[:], mv[:, :, 0], start=True, stop=True)
                if kind == "var":
                    pe.wait_ge(dev_ready, image + 1)
                    ins = nc.tensor.matmul(SD[:, bank, 0:CC], group_mean[:], vd, start=True, stop=True)
                ins.then_inc(side_filled, 1)
                cnt.passed(use)

            def scores(b, v, cnt):
                head, q, kp = v // 8, v // 4 % 2, v % 4
                slot = head_slot(head // 2, head % 2)
                if v % 8 == 0:
                    pe.wait_ge(side_drained, cnt.mark["shift"])
                wait(pe, exp_done, UNITS * b + v - 1)
                for i in range(2):
                    kb = bass.ts(2 * kp + i, P)
                    dst = ST[:, v % 2, bass.ts(i, HALF)]
                    nc.tensor.matmul(dst, K1[:, slot, kb], Q1[:, slot, bass.ts(q, HALF)], start=True, stop=False)
                    ins = nc.tensor.matmul(dst, K2[:, slot, kb], Q2[:, slot, bass.ts(q, HALF)], start=False,
                                           stop=True)
                ins.then_inc(scores_ready, 1)

            def times_v(b, v, i, cnt):
                head, kp = v // 8, v % 4
                if i == 0:
                    pe.wait_ge(exp_done, UNITS * b + v + 1)
                    if v % 2 == 0:
                        pe.wait_ge(lo_dve, 32 * b + v // 2 + 1)
                    else:
                        pe.wait_ge(lo_pool, 32 * b + v // 2 + 1)
                    if kp == 0:
                        wait(pe, pv_out, 16 * b + v // 4)
                    if v == 0:
                        pe.wait_ge(side_drained, cnt.mark["v"])
                    if v == 48:
                        pe.wait_ge(v_moved, b + 1)
                kb = 2 * kp + i
                for qb in range(4):
                    at = i * HALF + qb * P
                    start, end = kb == 0 and qb % 2 == 0, kb == TB - 1
                    nc.tensor.matmul(pv_blocks[:, qb // 2, qb % 2, 0:LO + HD], Ph[:, v % 4, at:at + P],
                                     V[:, kb, v_slot(head), 0:LO + HD], start=start, stop=end,
                                     skip_group_check=True)
                    ins = nc.tensor.matmul(pv_blocks[:, qb // 2, qb % 2, 0:LO], Pl[:, v % 4, at:at + P],
                                           V[:, kb, v_slot(head), 0:LO], start=False, stop=end,
                                           skip_group_check=True)
                if i == 1:
                    ins.then_inc(pv_done, 1)

            def step(b, s, cnt, first=False, last=False):
                for u in range(16):
                    v = 16 * s + u
                    uses = side_uses(s, u, first, last)
                    scores(b, v, cnt)
                    for use in uses[0:1]:
                        side(use, image_of(use, b, s), cnt)
                    if not (first and v < 2):
                        before = (b, v - 2) if v >= 2 else (b - 1, UNITS + v - 2)
                        times_v(*before, 0, cnt)
                    for use in uses[1:2]:
                        side(use, image_of(use, b, s), cnt)
                    if not (first and v < 2):
                        times_v(*before, 1, cnt)
                    for use in uses[2:]:
                        side(use, image_of(use, b, s), cnt)

            cnt = Count()
            for use in PROLOGUE:
                side(use, 0, cnt)
            step(0, 0, cnt, first=True)
            with pe.Fori(0, B - 1) as b:
                now = cnt.later(b)
                for s in (1, 2, 3):
                    step(b, s, now)
                step(b + 1, 0, now)
            now = cnt.later(B - 1)
            for s in (1, 2, 3):
                step(B - 1, s, now, last=True)
            for v in (UNITS - 2, UNITS - 1):
                times_v(B - 1, v, 0, now)
                times_v(B - 1, v, 1, now)
            for use in EPILOGUE:
                side(use, B - 1, now)


_INS = ["x", "L0_conv_gn_scale", "L0_conv_gn_offset", "L0_conv_w_qkv", "L0_conv_w_out", "L0_conv_b_out"]


def kernel(**inputs):
    import concourse.bacc as bacc
    from concourse.bass_utils import run_bass_kernel_spmd as run

    nc = bacc.Bacc("TRN2", target_bir_lowering=False, num_devices=1)
    arrays, args = {}, []
    for name in _INS:
        a = np.ascontiguousarray(inputs[name])
        arrays[f"in_{name}"] = a
        args.append(nc.dram_tensor(f"in_{name}", a.shape, mybir.dt.from_np(a.dtype), kind="ExternalInput").ap())
    args.append(nc.dram_tensor("out_0", (B, 32, 32, CH), F32, kind="ExternalOutput").ap())
    conv_attention(nc, *args)
    return run(nc, [arrays], core_ids=[0]).results[0]["out_0"]
```

```python
import numpy as np
import concourse.bass as bass
from concourse import mybir
from contextlib import ExitStack

F32, F16, I32 = mybir.dt.float32, mybir.dt.float16, mybir.dt.int32
ACT = mybir.ActivationFunctionType
ALU = mybir.AluOpType
AX = mybir.AxisListType

P = 128
B, TOK, CH = 16, 1024, 512
HEADS, HD = 8, 64
GROUP = 16
EPS = 1e-5
CC = CH // P
TB = TOK // P
HALF = 512
VW = 130
LO = HD + 1
UNITS = 64
TOP = 2.0 ** 14
ROWC = 2.0 ** 15
SHIFT_UP = 8 * float(np.log(2.0))
EXPONENT = 0x7F800000
RSQRT_GUESS = float(0x5F3759DF)
NEWTON = 3
NORMED_MAX = float(GROUP * TOK) ** 0.5
Q_SCALE, K_SCALE, V_SCALE = 3, 4, 5
DVE_STEPS = 7
MAX_PER_W = [3, 2, 3, 2, 3, 2, 1, 0]


def head_slot(pair, hh):
    return (pair % 2) * 2 + hh


def rows_of(hh):
    return slice(hh * HD, hh * HD + HD)


def v_slot(head):
    return head + 2 if head < 6 else head - 6


def top_uses(step, u, last=False):
    w, hh = u % 8, u // 8
    nxt = (step, 1) if hh == 0 else ((step + 1) % 4, 0)
    if last and step == 3 and hh == 1:
        return []
    if w == 7:
        return [("shift", *nxt, 0), ("shift", *nxt, 1)]
    done = sum(MAX_PER_W[:w])
    return [("max", *nxt, i // 2, i % 2) for i in range(done, done + MAX_PER_W[w])]


def side_uses(step, u, first=False, last=False):
    if u in (0, 2, 4, 6) and not (last and step == 3):
        return [("qk", (step + 1) % 4, "qk"[u // 2 % 2], u // 4)]
    if u in (3, 5) and not (first and step == 0):
        return [("ot", (step - 1) % 4, u // 4)]
    if step == 0 and u >= 8 and not first:
        return [("out", u - 8)]
    if step == 1 and u >= 8 and not last:
        return [("xt", u - 8)]
    if step == 2 and u in (7, 8) and not last:
        return [("mean",) if u == 7 else ("var",)]
    if step == 3 and u >= 8 and not last:
        return [("v", u - 8)]
    return []


def side_before(step, u, first=False, last=False):
    if u > 0:
        return side_uses(step, u - 1, first, last)
    return side_uses(step - 1, 15, last=last) if step > 1 else [] if first or step == 1 else side_uses(3, 15)


def image_of(use, b, step):
    if use[0] in ("xt", "mean", "var", "v") or (use[0] == "qk" and step == 3):
        return b + 1
    if use[0] == "out" or (use[0] == "ot" and step == 0):
        return b - 1
    return b


def image_before(use, b, step, u):
    return image_of(use, b, step) if u > 0 else image_of(use, b, step - 1) if step > 0 else b


PROLOGUE = ([("xt", t) for t in range(TB)] + [("mean",), ("var",)]
            + [("qk", 0, "qk"[i % 2], i // 2) for i in range(4)] + [("v", t) for t in range(TB)])
TOP_PROLOGUE = [("max", 0, 0, i // 2, i % 2) for i in range(16)] + [("shift", 0, 0, 0), ("shift", 0, 0, 1)]
EPILOGUE = [("ot", 3, 0), ("ot", 3, 1)] + [("out", t) for t in range(TB)]
IMAGE_USES = [x for s in range(4) for u in range(16) for x in side_uses(s, u)]
HI_PARTS = {"qk": 2, "v": 1, "ot": 1}


class Count:
    PER_IMAGE = {"side": len(IMAGE_USES), "hi": sum(HI_PARTS.get(x[0], 0) for x in IMAGE_USES),
                 "top": HEADS * 18, "heads": HEADS}

    def __init__(self, side=0, hi=0, top=0, heads=0, mark=None):
        self.side, self.hi, self.top, self.heads = side, hi, top, heads
        self.mark = dict(mark or {"qk": 0, "v": 0, "ot": 0})

    def passed(self, use):
        if use[0] in ("max", "shift"):
            self.top = self.top + 1
            if use[0] == "shift" and use[3] == 1:
                self.heads = self.heads + 1
            return
        self.side = self.side + 1
        self.hi = self.hi + HI_PARTS.get(use[0], 0)
        if use[0] in self.mark:
            self.mark[use[0]] = self.side

    def later(self, images):
        n = {name: images * per for name, per in self.PER_IMAGE.items()}
        return Count(self.side + n["side"], self.hi + n["hi"], self.top + n["top"], self.heads + n["heads"],
                     {kind: at + n["side"] for kind, at in self.mark.items()})


def wait(eng, sem, count):
    if not isinstance(count, int) or count > 0:
        eng.wait_ge(sem, count)


def conv_attention(nc, x, gamma, beta, w_qkv, w_out, b_out, out):
    x_blocks = x.rearrange("b h w c -> (b h w) c").rearrange("(n p) c -> n p c", p=P)
    out_blocks = out.rearrange("b h w c -> (b h w) c").rearrange("(n p) c -> n p c", p=P)

    ctx = ExitStack()
    with ctx:
        def sb(name, shape, dt):
            return ctx.enter_context(nc.sbuf_tensor(name, shape, dt))

        def ps(name, shape, dt):
            return ctx.enter_context(nc.psum_tensor(name, shape, dt))

        def sem(name):
            return ctx.enter_context(nc.semaphore(name))

        ident32 = sb("ident32", [P, P], F32)
        ident16 = sb("ident16", [P, P], F16)
        group_mean = sb("group_mean", [P, P], F32)
        gam = sb("gam", [P, CC], F32)
        bet = sb("bet", [P, CC], F32)
        bias = sb("bias", [P, CH], F32)
        wq = sb("wq", [P, 2, CC, 3 * CH], F16)
        wo = sb("wo", [P, 2, CC, CH], F16)
        red = sb("red", [P, 8], F32)
        top = sb("top", [P, 8], F32)
        pw = sb("pw", [P, 8], F32)
        sc = sb("sc", [P, 8], F32)
        inv = sb("inv", [P, 8], F32)
        tot = sb("tot", [P, 8], F32)
        cns = sb("cns", [P, 4], F32)
        absg = sb("absg", [P, CC], F32)
        absb = sb("absb", [P, CC], F32)
        bound = sb("bound", [P, CC], F32)
        bound16 = sb("bound16", [P, CC], F16)
        x_in = sb("x_in", [P, 2, CH], F32)
        work = sb("work", [P, 6 * TOK], F32)
        xT = work[:, 0:4 * TOK].rearrange("p (c n) -> p c n", c=CC)
        z = work[:, 4 * TOK:5 * TOK]
        th = work[:, 5 * TOK:6 * TOK]
        st = sb("st", [P, CC, 12], F32)
        mv = sb("mv", [P, CC, 2], F32)
        gn = sb("gn", [P, 16, CC], F32)
        gmean, dev, dev2, vd, veps, half_v, three_halves, half_bits, root, a_c, ma_c, b_c, ah, bh, az, bz = (
            gn[:, i, :] for i in range(16))
        nt = sb("nt", [P, 2, CC], F32)
        xn = sb("xn", [P, 2, CC, TOK], F16)
        K1 = sb("K1", [P, 4, TOK], F16)
        K2 = sb("K2", [P, 4, TOK], F16)
        Q1 = sb("Q1", [P, 4, TOK], F16)
        Q2 = sb("Q2", [P, 4, TOK], F16)
        V = sb("V", [P, TB, 10, VW], F16)
        mx = sb("mx", [P, 2, TB, 2], F32)
        mx8 = sb("mx8", [P, TB], F32)
        ms = sb("ms", [P, 2, TB], F16)
        P32 = sb("P32", [P, 2, 2 * HALF], F32)
        Ph = sb("Ph", [P, 4, 2 * HALF], F16)
        Pl = sb("Pl", [P, 4, 2 * HALF], F16)
        pv_lo = sb("pv_lo", [P, 2, 4, HD], F32)
        pv_sum = sb("pv_sum", [P, 2, 4, HD], F32)
        den = sb("den", [P, 2, 4], F32)
        O32 = sb("O32", [P, 2, TB, P], F32)
        OT = sb("OT", [P, 2, CC, TOK], F16)
        res = sb("res", [P, 4, CH], F32)

        w_stage = work[:, :].rearrange("p (c n) -> p c n", c=CC)
        wo_stage = P32[:, :, :].rearrange("p a b -> p (a b)").rearrange("p (c n) -> p c n", c=CC)
        w_abs = xn[:, :, :, :].rearrange("p a c n -> p (a c n)")[:, 0:CC * 3 * CH].rearrange(
            "p (c n) -> p c n", c=CC)

        ST = ps("ST", [P, 2, 2 * HALF], F32)
        PV = ps("PV", [P, 2, 512], F32)
        SD = ps("SD", [P, 512], F32)
        TP = ps("TP", [P, 512], F32)

        bound_psum = ST[:, :, :].rearrange("p a (b n) -> p (a b) n", n=512)
        pv_blocks = PV[:, :, 0:2 * (LO + HD)].rearrange("p a (q c) -> p a q c", q=2)

        w_loaded = sem("w_loaded")
        const_ready = sem("const_ready")
        maxima_in = sem("maxima_in")
        maxima_out = sem("maxima_out")
        setup_step = sem("setup_step")
        bound_in = sem("bound_in")
        bound_out = sem("bound_out")
        setup_done = sem("setup_done")
        x_loaded = [sem(f"x_loaded{i}") for i in range(2)]
        res_loaded = [sem(f"res_loaded{i}") for i in range(4)]
        res_biased = sem("res_biased")
        stored = [sem(f"stored{i}") for i in range(4)]
        side_filled = sem("side_filled")
        side_hi = sem("side_hi")
        side_drained = sem("side_drained")
        top_filled = sem("top_filled")
        top_drained = sem("top_drained")
        bn_done = sem("bn_done")
        chan_stats = sem("chan_stats")
        dve_step = sem("dve_step")
        dev_ready = sem("dev_ready")
        guess_ready = sem("guess_ready")
        newton_step = sem("newton_step")
        coef_ready = sem("coef_ready")
        silu_ready = sem("silu_ready")
        xn_f32 = sem("xn_f32")
        xn_hi = sem("xn_hi")
        xn_lo = sem("xn_lo")
        v_moved = sem("v_moved")
        mx8_ready = sem("mx8_ready")
        shift_ready = sem("shift_ready")
        scores_ready = sem("scores_ready")
        exp_done = sem("exp_done")
        lo_dve = sem("lo_dve")
        lo_pool = sem("lo_pool")
        pv_done = sem("pv_done")
        pv_lo_out = sem("pv_lo_out")
        pv_out = sem("pv_out")
        o_normed = sem("o_normed")

        block = ctx.enter_context(nc.Block())

        @block.sync
        def _(sp):
            sp.dma_start(w_stage, w_qkv.rearrange("(c p) n -> p c n", p=P)).then_inc(w_loaded, 16)
            sp.dma_start(wo_stage, w_out.rearrange("(c p) n -> p c n", p=P)).then_inc(w_loaded, 16)
            sp.dma_start(gam[:], gamma.rearrange("(c p) -> p c", p=P), allow_slow_non_contiguous=True).then_inc(w_loaded, 16)
            sp.dma_start(bet[:], beta.rearrange("(c p) -> p c", p=P), allow_slow_non_contiguous=True).then_inc(w_loaded, 16)
            sp.dma_start(bias[:], b_out.rearrange("(o c) -> o c", o=1).to_broadcast([P, CH])
                         ).then_inc(w_loaded, 16)

            def load_x(image, t, filled):
                src = x_blocks[bass.ds(sp.snap(image * TB + t), 1)].rearrange("o p c -> p (o c)")
                wait(sp, side_filled, filled)
                sp.dma_start(x_in[:, t % 2, :], src).then_inc(x_loaded[t % 2], 16)

            def load_res(image, t):
                src = x_blocks[bass.ds(sp.snap(image * TB + t), 1)].rearrange("o p c -> p (o c)")
                wait(sp, stored[t % 4], 32 * image + 16 * (t // 4))
                sp.dma_start(res[:, t % 4, :], src).then_inc(res_loaded[t % 4], 16)

            def store(image, t, drained):
                dst = out_blocks[bass.ds(sp.snap(image * TB + t), 1)].rearrange("o p c -> p (o c)")
                wait(sp, side_drained, drained)
                sp.dma_start(dst, res[:, t % 4, :]).then_inc(stored[t % 4], 16)

            def step(b, s, cnt, first=False, last=False):
                filled = [cnt.side, cnt.side]
                if s == 1:
                    for t in range(4):
                        load_res(b, t)
                for u in range(16):
                    for use in side_uses(s, u, first, last):
                        cnt.passed(use)
                        if use[0] == "xt":
                            load_x(b + 1, use[1], filled[use[1]])
                            filled.append(cnt.side)
                        if use[0] == "out":
                            store(b - 1, use[1], cnt.side)
                            if use[1] < 4:
                                load_res(b - 1, use[1] + 4)

            cnt = Count()
            for use in PROLOGUE:
                cnt.passed(use)
                if use[0] == "xt":
                    load_x(0, use[1], use[1] - 1)
            step(0, 0, cnt, first=True)
            with sp.Fori(0, B - 1) as b:
                now = cnt.later(b)
                for s in (1, 2, 3):
                    step(b, s, now)
                step(b + 1, 0, now)
            now = cnt.later(B - 1)
            for s in (1, 2, 3):
                step(B - 1, s, now, last=True)
            for use in EPILOGUE:
                now.passed(use)
                if use[0] == "out":
                    store(B - 1, use[1], now.side)
                    if use[1] < 4:
                        load_res(B - 1, use[1] + 4)
            for t in range(4):
                sp.wait_ge(stored[t], 32 * B)

        @block.gpsimd
        def _(pool):
            nc.gpsimd.memset(ident32[:], 0.0).then_inc(const_ready, 1)
            nc.gpsimd.memset(group_mean[:], 1.0 / GROUP).then_inc(const_ready, 1)
            pool.wait_ge(const_ready, 2)
            nc.gpsimd.affine_select(out=ident32[:], in_=ident32[:], compare_op=ALU.not_equal, fill=1.0, base=0,
                                    pattern=[[-1, P]], channel_multiplier=1).then_inc(const_ready, 1)
            grouped = group_mean[:].rearrange("p (g c) -> p g c", c=GROUP)
            nc.gpsimd.affine_select(out=grouped, in_=grouped, compare_op=ALU.is_ge, fill=0.0, base=0,
                                    pattern=[[-GROUP, P // GROUP], [0, GROUP]], channel_multiplier=1
                                    ).then_inc(const_ready, 1)
            pool.wait_ge(const_ready, 4)
            nc.gpsimd.affine_select(out=grouped, in_=grouped, compare_op=ALU.is_ge, fill=0.0, base=GROUP - 1,
                                    pattern=[[GROUP, P // GROUP], [0, GROUP]], channel_multiplier=-1
                                    ).then_inc(const_ready, 1)
            pool.wait_ge(maxima_in, 1)
            nc.gpsimd.partition_all_reduce(top[:, 0:3], red[:, 0:3], P, bass.bass_isa.ReduceOp.max
                                           ).then_inc(maxima_out, 1)
            pool.wait_ge(setup_done, 1)

            def newton(image):
                n = 4 * NEWTON * image
                pool.wait_ge(guess_ready, image + 1)
                for i in range(0, 4 * NEWTON, 4):
                    nc.gpsimd.tensor_tensor(nt[:, 0, :], root, root, ALU.mult).then_inc(newton_step, 1)
                    pool.wait_ge(newton_step, n + i + 1)
                    nc.gpsimd.tensor_tensor(nt[:, 1, :], nt[:, 0, :], half_v, ALU.mult).then_inc(newton_step, 1)
                    pool.wait_ge(newton_step, n + i + 2)
                    nc.gpsimd.tensor_tensor(nt[:, 0, :], three_halves, nt[:, 1, :], ALU.subtract
                                            ).then_inc(newton_step, 1)
                    pool.wait_ge(newton_step, n + i + 3)
                    nc.gpsimd.tensor_tensor(root, root, nt[:, 0, :], ALU.mult).then_inc(newton_step, 1)
                    pool.wait_ge(newton_step, n + i + 4)

            def low_xn(image, c):
                pool.wait_ge(xn_hi, 4 * image + c + 1)
                nc.gpsimd.tensor_tensor(xn[:, 1, c, :], xT[:, c, :], xn[:, 0, c, :], ALU.subtract
                                        ).then_inc(xn_lo, 1)

            def add_bias(image, t):
                pool.wait_ge(res_loaded[t % 4], 32 * image + 16 * (t // 4) + 16)
                nc.gpsimd.tensor_tensor(res[:, t % 4, :], res[:, t % 4, :], bias[:], ALU.add
                                        ).then_inc(res_biased, 1)

            def low_probs(b, v):
                pool.wait_ge(exp_done, UNITS * b + v + 1)
                wait(pool, pv_done, UNITS * b + v - 3)
                nc.gpsimd.tensor_tensor(Pl[:, v % 4, :], P32[:, v % 2, :], Ph[:, v % 4, :], ALU.subtract
                                        ).then_inc(lo_pool, 1)

            def normalise(b, half):
                pool.wait_ge(pv_out, 16 * b + half + 1)
                pair, hh, q = half // 4 % 4, half // 2 % 2, half % 2
                nc.gpsimd.tensor_tensor(O32[:, pair % 2, 4 * q:4 * q + 4, rows_of(hh)], pv_sum[:, half % 2],
                                        den[:, half % 2, :].unsqueeze(2).to_broadcast([P, 4, HD]), ALU.mult
                                        ).then_inc(o_normed, 1)

            def step(b, s, first=False, last=False):
                for u in range(16):
                    v = 16 * s + u
                    if v % 2 == 0 and not (first and v == 0):
                        low_probs(b, v - 1)
                    if v % 4 == 1 and not (first and v == 1):
                        normalise(b, v // 4 - 1)
                    if s == 2 and u == 9 and not last:
                        newton(b + 1)
                    if s == 2 and u >= 12 and not last:
                        low_xn(b + 1, u - 12)
                    if s == 3 and u < 4:
                        add_bias(b, u)
                    if s == 0 and 11 <= u < 15 and not first:
                        add_bias(b - 1, u - 7)

            newton(0)
            for c in range(CC):
                low_xn(0, c)
            step(0, 0, first=True)
            with pool.Fori(0, B - 1) as b:
                for s in (1, 2, 3):
                    step(b, s)
                step(b + 1, 0)
            for s in (1, 2, 3):
                step(B - 1, s, last=True)
            low_probs(B - 1, UNITS - 1)
            normalise(B - 1, 15)
            for t in range(4, 8):
                add_bias(B - 1, t)

        @block.scalar
        def _(act):
            act.wait_ge(setup_done, 1)

            def side(use, image, cnt):
                if use[0] in HI_PARTS:
                    act.wait_ge(side_filled, cnt.side + 1)
                if use[0] == "qk":
                    _, pair, which, half = use
                    dst, col = (Q1, Q_SCALE) if which == "q" else (K1, K_SCALE)
                    for hh in range(2):
                        r = rows_of(hh)
                        nc.scalar.activation(dst[r, head_slot(pair, hh), bass.ts(half, HALF)], SD[r, :],
                                             ACT.Identity, scale=sc[r, col:col + 1]).then_inc(side_hi, 1)
                if use[0] == "v":
                    wait(act, v_moved, image)
                    nc.scalar.activation(V[:, use[1], 2:10, 0:HD],
                                         SD[:].rearrange("p (h d) -> p h d", d=HD), ACT.Identity,
                                         scale=sc[:, V_SCALE:V_SCALE + 1]).then_inc(side_hi, 1)
                if use[0] == "ot":
                    _, pair, half = use
                    nc.scalar.activation(OT[:, 0, pair, bass.ts(half, HALF)], SD[:], ACT.Copy
                                         ).then_inc(side_hi, 1)
                cnt.passed(use)

            def silu_parts(image, c):
                act.wait_ge(coef_ready, image + 1)
                wait(act, xn_f32, 4 * image + c)
                nc.scalar.activation(z, xT[:, c, :], ACT.Identity, scale=az[:, c:c + 1], bias=bz[:, c:c + 1])
                nc.scalar.activation(th, xT[:, c, :], ACT.Tanh, scale=ah[:, c:c + 1], bias=bh[:, c:c + 1]
                                     ).then_inc(silu_ready, 1)

            def exponentials(b, v):
                act.wait_ge(scores_ready, UNITS * b + v + 1)
                if v % 2 == 0:
                    wait(act, lo_dve, 32 * b + v // 2)
                else:
                    wait(act, lo_pool, 32 * b + v // 2)
                nc.scalar.activation(P32[:, v % 2, :], ST[:, v % 2, :], ACT.Exp, scale=cns[:, 0:1])
                wait(act, pv_done, UNITS * b + v - 3)
                nc.scalar.activation(Ph[:, v % 4, :], ST[:, v % 2, :], ACT.Exp, scale=cns[:, 0:1]
                                     ).then_inc(exp_done, 1)

            def low_sums(b, half):
                act.wait_ge(pv_done, UNITS * b + 4 * half + 4)
                wait(act, pv_out, 16 * b + half - 1)
                nc.scalar.activation(pv_lo[:, half % 2].rearrange("p (a q) d -> p a q d", a=2),
                                     pv_blocks[:, :, :, LO:LO + HD], ACT.Copy).then_inc(pv_lo_out, 1)

            def step(b, s, cnt, first=False, last=False):
                for u in range(16):
                    v = 16 * s + u
                    for use in side_before(s, u, first, last):
                        side(use, image_before(use, b, s, u), cnt)
                    exponentials(b, v)
                    if v % 4 == 1 and not (first and v == 1):
                        low_sums(b, v // 4 - 1)
                    if s == 2 and 11 <= u < 15 and not last:
                        silu_parts(b + 1, u - 11)
                    if s == 0 and u == 15:
                        for use in side_uses(s, u, first, last):
                            side(use, image_of(use, b, s), cnt)

            cnt = Count()
            for use in PROLOGUE:
                side(use, 0, cnt)
                if use[0] == "var":
                    for c in range(CC):
                        silu_parts(0, c)
            step(0, 0, cnt, first=True)
            with act.Fori(0, B - 1) as b:
                now = cnt.later(b)
                for s in (1, 2, 3):
                    step(b, s, now)
                step(b + 1, 0, now)
            now = cnt.later(B - 1)
            for s in (1, 2, 3):
                step(B - 1, s, now, last=True)
            low_sums(B - 1, 15)
            for use in EPILOGUE:
                side(use, B - 1, now)

        @block.vector
        def _(dve):
            steps = [0]

            def then(ins):
                steps[0] += 1
                ins.then_inc(setup_step, 1)
                dve.wait_ge(setup_step, steps[0])

            def scale_of(dst, inverse, size):
                n = size.shape[1]
                then(nc.vector.tensor_scalar(size, size, 1e-30, None, ALU.max))
                then(nc.vector.tensor_scalar(pw[:, 0:n].bitcast(I32), size.bitcast(I32), EXPONENT, None,
                                             ALU.bitwise_and))
                then(nc.vector.tensor_scalar(inverse, pw[:, 0:n], 1.0 / TOP, None, ALU.mult))
                then(nc.vector.reciprocal(dst, inverse))

            nc.vector.memset(V[:], 1.0)
            nc.vector.memset(K2[:], ROWC)
            nc.vector.memset(three_halves, 1.5)
            dve.wait_ge(const_ready, 5)
            nc.vector.tensor_copy(ident16[:], ident32[:])
            dve.wait_ge(w_loaded, 16 * 5)
            then(nc.vector.tensor_reduce(red[:, 0:1], w_stage, AX.XY, ALU.max, apply_absolute_value=True))
            then(nc.vector.tensor_reduce(red[:, 1:2], wo_stage, AX.XY, ALU.max, apply_absolute_value=True))
            then(nc.vector.scalar_tensor_tensor(out=absg[:], in0=gam[:], scalar=-1.0, in1=gam[:],
                                                op0=ALU.mult, op1=ALU.max))
            then(nc.vector.scalar_tensor_tensor(out=absb[:], in0=bet[:], scalar=-1.0, in1=bet[:],
                                                op0=ALU.mult, op1=ALU.max))
            then(nc.vector.scalar_tensor_tensor(out=bound[:], in0=absg[:], scalar=NORMED_MAX, in1=absb[:],
                                                op0=ALU.mult, op1=ALU.add))
            nc.vector.tensor_reduce(red[:, 2:3], bound[:], AX.X, ALU.max).then_inc(maxima_in, 1)
            dve.wait_ge(maxima_out, 1)
            scale_of(sc[:, 0:3], inv[:, 0:3], top[:, 0:3])
            then(nc.vector.tensor_scalar(wq[:, 0], w_stage, sc[:, 0:1], None, ALU.mult))
            then(nc.vector.scalar_tensor_tensor(out=wq[:, 1], in0=w_stage, scalar=sc[:, 0:1], in1=wq[:, 0],
                                                op0=ALU.mult, op1=ALU.subtract))
            then(nc.vector.tensor_scalar(wo[:, 0], wo_stage, sc[:, 1:2], None, ALU.mult))
            then(nc.vector.scalar_tensor_tensor(out=wo[:, 1], in0=wo_stage, scalar=sc[:, 1:2], in1=wo[:, 0],
                                                op0=ALU.mult, op1=ALU.subtract))
            then(nc.vector.scalar_tensor_tensor(out=w_abs, in0=wq[:, 0], scalar=-1.0, in1=wq[:, 0],
                                                op0=ALU.mult, op1=ALU.max))
            nc.vector.tensor_scalar(bound16[:], bound[:], sc[:, 2:3], None, ALU.mult).then_inc(bound_in, 1)
            dve.wait_ge(bound_out, 1)
            for i in range(3):
                then(nc.vector.tensor_reduce(top[:, 3 + i:4 + i], bound_psum[:, i, :], AX.X, ALU.max))
            scale_of(sc[:, 3:6], inv[:, 3:6], top[:, 3:6])
            then(nc.vector.tensor_scalar(tot[:, 0:3], inv[:, 3:6], inv[:, 0:1], inv[:, 2:3], ALU.mult, ALU.mult))
            then(nc.vector.tensor_scalar(cns[:, 0:1], tot[:, 0:1], tot[:, 1:2], HD ** -0.5, ALU.mult, ALU.mult))
            then(nc.vector.tensor_scalar(cns[:, 1:2], tot[:, 2:3], inv[:, 1:2], None, ALU.mult))
            then(nc.vector.reciprocal(cns[:, 2:3], cns[:, 0:1]))
            nc.vector.tensor_scalar(cns[:, 3:4], cns[:, 2:3], SHIFT_UP, None, ALU.mult).then_inc(setup_done, 1)
            dve.wait_ge(setup_done, 1)

            def side(use, image, cnt):
                kind = use[0]
                dve.wait_ge(side_filled, cnt.side + 1)
                if kind in HI_PARTS:
                    dve.wait_ge(side_hi, cnt.hi + 1)
                if kind == "qk":
                    _, pair, which, half = use
                    cols = bass.ts(half, HALF)
                    for hh in range(2):
                        r, other, slot = rows_of(hh), rows_of(1 - hh), head_slot(pair, hh)
                        hi, lo, col = ((Q1[r, slot, cols], Q2[r, slot, cols], Q_SCALE) if which == "q" else
                                       (K1[r, slot, cols], K1[other, slot, cols], K_SCALE))
                        if hh == 1:
                            dve.wait_ge(side_hi, cnt.hi + 2)
                        low = nc.vector.scalar_tensor_tensor(out=lo, in0=SD[r, :], scalar=sc[r, col:col + 1],
                                                             in1=hi, op0=ALU.mult, op1=ALU.subtract)
                    low.then_inc(side_drained, 1)
                    for hh in range(2):
                        r, other, slot = rows_of(hh), rows_of(1 - hh), head_slot(pair, hh)
                        if which == "q":
                            nc.vector.tensor_copy(Q1[other, slot, cols], Q1[r, slot, cols])
                        else:
                            nc.vector.tensor_copy(K2[r, slot, cols], K1[r, slot, cols])
                if kind == "v":
                    wait(dve, v_moved, image)
                    nc.vector.scalar_tensor_tensor(
                        out=V[:, use[1], 2:10, LO:LO + HD], in0=SD[:].rearrange("p (h d) -> p h d", d=HD),
                        scalar=sc[:, V_SCALE:V_SCALE + 1], in1=V[:, use[1], 2:10, 0:HD],
                        op0=ALU.mult, op1=ALU.subtract).then_inc(side_drained, 1)
                if kind == "ot":
                    _, pair, half = use
                    cols = bass.ts(half, HALF)
                    nc.vector.tensor_tensor(OT[:, 1, pair, cols], SD[:], OT[:, 0, pair, cols],
                                            ALU.subtract).then_inc(side_drained, 1)
                if kind == "out":
                    dve.wait_ge(res_biased, TB * image + use[1] + 1)
                    nc.vector.scalar_tensor_tensor(out=res[:, use[1] % 4, :], in0=SD[:],
                                                   scalar=cns[:, 1:2], in1=res[:, use[1] % 4, :],
                                                   op0=ALU.mult, op1=ALU.add).then_inc(side_drained, 1)
                if kind == "xt":
                    wait(dve, xn_lo, CC * image)
                    wait(dve, xn_hi, CC * image)
                    nc.vector.tensor_copy(xT[:, :, bass.ts(use[1], P)],
                                          SD[:].rearrange("p (c n) -> p c n", c=CC)
                                          ).then_inc(side_drained, 1)
                if kind == "mean":
                    n = DVE_STEPS * image
                    nc.vector.tensor_copy(gmean, SD[:, 0:CC]).then_inc(side_drained, 1)
                    dve.wait_ge(side_drained, cnt.side + 1)
                    nc.vector.tensor_tensor(dev, mv[:, :, 0], gmean, ALU.subtract).then_inc(dve_step, 1)
                    dve.wait_ge(dve_step, n + 1)
                    nc.vector.tensor_tensor(dev2, dev, dev, ALU.mult).then_inc(dve_step, 1)
                    dve.wait_ge(dve_step, n + 2)
                    nc.vector.tensor_tensor(vd, dev2, mv[:, :, 1], ALU.add).then_inc(dev_ready, 1)
                if kind == "var":
                    n = DVE_STEPS * image + 2
                    nc.vector.tensor_scalar(veps, SD[:, 0:CC], EPS, None, ALU.add
                                            ).then_inc(side_drained, 1)
                    dve.wait_ge(side_drained, cnt.side + 1)
                    nc.vector.tensor_scalar(half_v, veps, 0.5, None, ALU.mult)
                    nc.vector.tensor_scalar(half_bits.bitcast(I32), veps.bitcast(I32), 1, None,
                                            ALU.logical_shift_right).then_inc(dve_step, 1)
                    dve.wait_ge(dve_step, n + 1)
                    nc.vector.tensor_scalar(root.bitcast(I32), half_bits.bitcast(I32), -1.0, RSQRT_GUESS,
                                            ALU.mult, ALU.add).then_inc(guess_ready, 1)
                cnt.passed(use)

            def shifts(hh, cnt):
                dve.wait_ge(top_drained, cnt.top)
                nc.vector.tensor_reduce(mx8[:], mx[:, hh], AX.X, ALU.max).then_inc(mx8_ready, 1)
                dve.wait_ge(mx8_ready, cnt.heads + 1)
                nc.vector.tensor_scalar(ms[:, hh, :], mx8[:], cns[:, 3:4], -1.0 / (HD * ROWC),
                                        ALU.subtract, ALU.mult).then_inc(shift_ready, 1)

            def top_use(use, cnt):
                dve.wait_ge(top_filled, cnt.top + 1)
                if use[0] == "max":
                    _, pair, hh, qb, kh = use
                    nc.vector.reduce_max(mx[:, hh, qb, kh:kh + 1], TP[:], AX.X).then_inc(top_drained, 1)
                else:
                    _, pair, hh, half = use
                    r = rows_of(1 - hh)
                    nc.vector.tensor_copy(Q2[r, head_slot(pair, hh), bass.ts(half, HALF)], TP[r, :]
                                          ).then_inc(top_drained, 1)
                cnt.passed(use)
                if use[0] == "max" and use[3:] == (TB - 1, 1):
                    shifts(use[2], cnt)

            def channel_stats(image, i, cnt):
                dve.wait_ge(side_drained, cnt.side)
                c, half = i // 2, i % 2
                stats = nc.vector.bn_stats(st[:, c, 6 * half:6 * half + 6], xT[:, c, bass.ts(half, HALF)])
                if i == 7:
                    stats.then_inc(bn_done, 1)

            def aggregate(image):
                for c in range(CC):
                    aggr = nc.vector.bn_aggr(mv[:, c, :], st[:, c, :])
                aggr.then_inc(chan_stats, 1)
                dve.wait_ge(chan_stats, image + 1)

            def coefficients(image):
                n = DVE_STEPS * image + 3
                dve.wait_ge(newton_step, 4 * NEWTON * (image + 1))
                nc.vector.tensor_tensor(a_c, gam[:], root, ALU.mult).then_inc(dve_step, 1)
                dve.wait_ge(dve_step, n + 1)
                nc.vector.tensor_tensor(ma_c, gmean, a_c, ALU.mult).then_inc(dve_step, 1)
                dve.wait_ge(dve_step, n + 2)
                nc.vector.tensor_tensor(b_c, bet[:], ma_c, ALU.subtract).then_inc(dve_step, 1)
                dve.wait_ge(dve_step, n + 3)
                nc.vector.tensor_scalar(ah, a_c, 0.5, None, ALU.mult)
                nc.vector.tensor_scalar(bh, b_c, 0.5, None, ALU.mult).then_inc(dve_step, 1)
                dve.wait_ge(dve_step, n + 4)
                nc.vector.tensor_scalar(az, ah, sc[:, 2:3], None, ALU.mult)
                nc.vector.tensor_scalar(bz, bh, sc[:, 2:3], None, ALU.mult).then_inc(coef_ready, 1)

            def silu(image, c):
                dve.wait_ge(silu_ready, CC * image + c + 1)
                nc.vector.scalar_tensor_tensor(out=xT[:, c, :], in0=th, scalar=1.0, in1=z,
                                               op0=ALU.add, op1=ALU.mult).then_inc(xn_f32, 1)
                dve.wait_ge(xn_f32, CC * image + c + 1)
                nc.vector.tensor_copy(xn[:, 0, c, :], xT[:, c, :]).then_inc(xn_hi, 1)

            def low_probs(b, v):
                dve.wait_ge(exp_done, UNITS * b + v + 1)
                wait(dve, pv_done, UNITS * b + v - 3)
                nc.vector.tensor_tensor(Pl[:, v % 4, :], P32[:, v % 2, :], Ph[:, v % 4, :], ALU.subtract
                                        ).then_inc(lo_dve, 1)

            def sums(b, half):
                dve.wait_ge(pv_lo_out, 16 * b + half + 1)
                wait(dve, o_normed, 16 * b + half - 1)
                nc.vector.reciprocal(den[:, half % 2, :].rearrange("p (a q) -> p a q", a=2),
                                     pv_blocks[:, :, :, HD])
                nc.vector.tensor_tensor(pv_sum[:, half % 2].rearrange("p (a q) d -> p a q d", a=2),
                                        pv_blocks[:, :, :, 0:HD],
                                        pv_lo[:, half % 2].rearrange("p (a q) d -> p a q d", a=2), ALU.add
                                        ).then_inc(pv_out, 1)

            def move_v(b, cnt):
                wait(dve, pv_done, UNITS * b)
                dve.wait_ge(side_drained, cnt.side)
                nc.vector.tensor_copy(V[:, :, 0:2, :], V[:, :, 8:10, :]).then_inc(v_moved, 1)

            def step(b, s, cnt, first=False, last=False):
                for u in range(16):
                    v = 16 * s + u
                    for use in side_before(s, u, first, last):
                        side(use, image_before(use, b, s, u), cnt)
                    tops = top_uses(s, u, last)
                    for use in tops[0:1]:
                        top_use(use, cnt)
                    if v % 2 == 1:
                        low_probs(b, v - 1)
                    for use in tops[1:]:
                        top_use(use, cnt)
                    if s == 0 and u == 15:
                        for use in side_uses(s, u, first, last):
                            side(use, image_of(use, b, s), cnt)
                    if v % 4 == 1 and not (first and v == 1):
                        sums(b, v // 4 - 1)
                    if s == 0 and u == 7:
                        move_v(b, cnt)
                    if s == 2 and not last:
                        if u < 4:
                            channel_stats(b + 1, 2 * u, cnt)
                            channel_stats(b + 1, 2 * u + 1, cnt)
                        if u == 5:
                            aggregate(b + 1)
                        if u == 10:
                            coefficients(b + 1)
                        if u >= 12:
                            silu(b + 1, u - 12)

            cnt = Count()
            for use in PROLOGUE:
                side(use, 0, cnt)
                if use == ("xt", TB - 1):
                    for i in range(8):
                        channel_stats(0, i, cnt)
                    dve.wait_ge(bn_done, 1)
                    aggregate(0)
                if use[0] == "var":
                    coefficients(0)
                    for c in range(CC):
                        silu(0, c)
            for use in TOP_PROLOGUE:
                top_use(use, cnt)
            step(0, 0, cnt, first=True)
            with dve.Fori(0, B - 1) as b:
                now = cnt.later(b)
                for s in (1, 2, 3):
                    step(b, s, now)
                step(b + 1, 0, now)
            now = cnt.later(B - 1)
            for s in (1, 2, 3):
                step(B - 1, s, now, last=True)
            sums(B - 1, 15)
            for use in EPILOGUE:
                side(use, B - 1, now)

        @block.tensor
        def _(pe):
            pe.wait_ge(bound_in, 1)
            for i in range(3):
                for c in range(CC):
                    last_mm = nc.tensor.matmul(bound_psum[:, i, :], bound16[:, c:c + 1].to_broadcast([P, P]),
                                               w_abs[:, c, i * CH:(i + 1) * CH], start=(c == 0),
                                               stop=(c == CC - 1))
            last_mm.then_inc(bound_out, 1)
            pe.wait_ge(setup_done, 1)

            SPLIT = ("qk", "v", "out")
            PASSES = [(c, i, j) for c in range(CC) for i, j in ((0, 0), (0, 1), (1, 0))]

            def three_passes(stationary, moving, part):
                for c, i, j in PASSES if part is None else PASSES[:6] if part == 0 else PASSES[6:]:
                    ins = nc.tensor.matmul(SD[:], stationary(i, c), moving(j, c),
                                           start=(c == 0 and i + j == 0), stop=(c == CC - 1 and i == 1))
                return ins

            def top_use(use, cnt):
                wait(pe, top_drained, cnt.top)
                if use[0] == "max":
                    _, pair, hh, qb, kh = use
                    r, slot = rows_of(hh), head_slot(pair, hh)
                    if qb == kh == 0:
                        wait(pe, side_drained, cnt.mark["qk"])
                    ins = nc.tensor.matmul(TP[:], Q1[r, slot, bass.ts(qb, P)], K1[r, slot, bass.ts(kh, HALF)],
                                           start=True, stop=True)
                else:
                    _, pair, hh, half = use
                    pe.wait_ge(shift_ready, cnt.heads + 1)
                    for i in range(4):
                        qb = 4 * half + i
                        ins = nc.tensor.matmul(TP[:, bass.ts(i, P)], ms[:, hh, qb:qb + 1].to_broadcast([P, P]),
                                               ident16[:], start=True, stop=True)
                ins.then_inc(top_filled, 1)
                cnt.passed(use)

            def side(use, image, cnt, part=None):
                kind = use[0]
                if part != 1:
                    wait(pe, side_drained, cnt.side)
                if kind == "qk":
                    _, pair, which, half = use
                    col = pair * P + (0 if which == "q" else CH)
                    if part != 1:
                        pe.wait_ge(xn_lo, CC * (image + 1))
                    ins = three_passes(lambda i, c: wq[:, i, c, col:col + P],
                                       lambda j, c: xn[:, j, c, bass.ts(half, HALF)], part)
                if kind == "v":
                    ins = three_passes(lambda i, c: xn[:, i, c, bass.ts(use[1], P)],
                                       lambda j, c: wq[:, j, c, 2 * CH:3 * CH], part)
                if kind == "out":
                    if part != 1:
                        pe.wait_ge(side_drained, cnt.mark["ot"])
                    ins = three_passes(lambda i, c: OT[:, i, c, bass.ts(use[1], P)],
                                       lambda j, c: wo[:, j, c, :], part)
                if part == 0:
                    return
                if kind == "ot":
                    _, pair, half = use
                    pe.wait_ge(o_normed, 16 * image + 4 * (pair + 1))
                    for i in range(4):
                        ins = nc.tensor.transpose(SD[:, bass.ts(i, P)], O32[:, pair % 2, 4 * half + i, :],
                                                  ident32[:])
                if kind == "xt":
                    t = use[1]
                    pe.wait_ge(x_loaded[t % 2], 16 * (TB // 2 * image + t // 2 + 1))
                    for c in range(CC):
                        ins = nc.tensor.transpose(SD[:, bass.ts(c, P)], x_in[:, t % 2, bass.ts(c, P)],
                                                  ident32[:])
                if kind == "mean":
                    pe.wait_ge(chan_stats, image + 1)
                    ins = nc.tensor.matmul(SD[:, 0:CC], group_mean[:], mv[:, :, 0], start=True, stop=True)
                if kind == "var":
                    pe.wait_ge(dev_ready, image + 1)
                    ins = nc.tensor.matmul(SD[:, 0:CC], group_mean[:], vd, start=True, stop=True)
                ins.then_inc(side_filled, 1)
                cnt.passed(use)

            def scores(b, v, i, cnt):
                head, q, kp = v // 8, v // 4 % 2, v % 4
                slot = head_slot(head // 2, head % 2)
                if i == 0:
                    if v % 8 == 0:
                        pe.wait_ge(top_drained, cnt.top)
                    wait(pe, exp_done, UNITS * b + v - 1)
                kb = bass.ts(2 * kp + i, P)
                dst = ST[:, v % 2, bass.ts(i, HALF)]
                nc.tensor.matmul(dst, K1[:, slot, kb], Q1[:, slot, bass.ts(q, HALF)], start=True, stop=False)
                ins = nc.tensor.matmul(dst, K2[:, slot, kb], Q2[:, slot, bass.ts(q, HALF)], start=False,
                                       stop=True)
                if i == 1:
                    ins.then_inc(scores_ready, 1)

            def times_v(b, v, i, cnt):
                head, kp = v // 8, v % 4
                if i == 0:
                    pe.wait_ge(exp_done, UNITS * b + v + 1)
                    if v % 2 == 0:
                        pe.wait_ge(lo_dve, 32 * b + v // 2 + 1)
                    else:
                        pe.wait_ge(lo_pool, 32 * b + v // 2 + 1)
                    if kp == 0:
                        wait(pe, pv_out, 16 * b + v // 4)
                    if v == 0:
                        pe.wait_ge(side_drained, cnt.mark["v"])
                    if v == 48:
                        pe.wait_ge(v_moved, b + 1)
                kb = 2 * kp + i
                for qb in range(4):
                    at = i * HALF + qb * P
                    start, end = kb == 0 and qb % 2 == 0, kb == TB - 1
                    nc.tensor.matmul(pv_blocks[:, qb // 2, qb % 2, 0:LO + HD], Ph[:, v % 4, at:at + P],
                                     V[:, kb, v_slot(head), 0:LO + HD], start=start, stop=end,
                                     skip_group_check=True)
                    ins = nc.tensor.matmul(pv_blocks[:, qb // 2, qb % 2, 0:LO], Pl[:, v % 4, at:at + P],
                                           V[:, kb, v_slot(head), 0:LO], start=False, stop=end,
                                           skip_group_check=True)
                if i == 1:
                    ins.then_inc(pv_done, 1)

            def step(b, s, cnt, first=False, last=False):
                for u in range(16):
                    v = 16 * s + u
                    sides, tops = side_uses(s, u, first, last), top_uses(s, u, last)
                    before = (b, v - 2) if v >= 2 else (b - 1, UNITS + v - 2)
                    scores(b, v, 0, cnt)
                    scores(b, v, 1, cnt)
                    for use in tops[0:1]:
                        top_use(use, cnt)
                    if not (first and v < 2):
                        times_v(*before, 0, cnt)
                        times_v(*before, 1, cnt)
                    for use in sides:
                        if use[0] in SPLIT:
                            side(use, image_of(use, b, s), cnt, part=0)
                    for use in tops[1:2]:
                        top_use(use, cnt)
                    for use in sides:
                        side(use, image_of(use, b, s), cnt, part=1 if use[0] in SPLIT else None)
                    for use in tops[2:]:
                        top_use(use, cnt)

            cnt = Count()
            for use in PROLOGUE:
                side(use, 0, cnt)
            for use in TOP_PROLOGUE:
                top_use(use, cnt)
            step(0, 0, cnt, first=True)
            with pe.Fori(0, B - 1) as b:
                now = cnt.later(b)
                for s in (1, 2, 3):
                    step(b, s, now)
                step(b + 1, 0, now)
            now = cnt.later(B - 1)
            for s in (1, 2, 3):
                step(B - 1, s, now, last=True)
            for v in (UNITS - 2, UNITS - 1):
                times_v(B - 1, v, 0, now)
                times_v(B - 1, v, 1, now)
            for use in EPILOGUE:
                side(use, B - 1, now)


_INS = ["x", "L0_conv_gn_scale", "L0_conv_gn_offset", "L0_conv_w_qkv", "L0_conv_w_out", "L0_conv_b_out"]


def kernel(**inputs):
    import concourse.bacc as bacc
    from concourse.bass_utils import run_bass_kernel_spmd as run

    nc = bacc.Bacc("TRN2", target_bir_lowering=False, num_devices=1)
    arrays, args = {}, []
    for name in _INS:
        a = np.ascontiguousarray(inputs[name])
        arrays[f"in_{name}"] = a
        args.append(nc.dram_tensor(f"in_{name}", a.shape, mybir.dt.from_np(a.dtype), kind="ExternalInput").ap())
    args.append(nc.dram_tensor("out_0", (B, 32, 32, CH), F32, kind="ExternalOutput").ap())
    conv_attention(nc, *args)
    return run(nc, [arrays], core_ids=[0]).results[0]["out_0"]
```

```python
import numpy as np
import concourse.bass as bass
from concourse import mybir
from contextlib import ExitStack

F32, F16, I32 = mybir.dt.float32, mybir.dt.float16, mybir.dt.int32
ACT = mybir.ActivationFunctionType
ALU = mybir.AluOpType
AX = mybir.AxisListType

P = 128
B, TOK, CH = 16, 1024, 512
HEADS, HD = 8, 64
GROUP = 16
EPS = 1e-5
CC = CH // P
TB = TOK // P
HALF = 512
VW = 130
LO = HD + 1
PV_COLS = 3 * (LO + HD) + LO
UNITS = 64
TOP = 2.0 ** 14
ROWC = 2.0 ** 15
PLACED = 6 * 16
SHIFT_UP = 8 * float(np.log(2.0))
EXPONENT = 0x7F800000
RSQRT_GUESS = float(0x5F3759DF)
NEWTON = 3
PIECES = 2 * CC
NORMED_MAX = float(GROUP * TOK) ** 0.5
Q_SCALE, K_SCALE, V_SCALE = 3, 4, 5
DVE_STEPS = 7
TOPS_PER_W = [3, 2, 3, 2, 3, 2, 2, 1]


def head_slot(pair, hh):
    return (pair % 2) * 2 + hh


def rows_of(hh):
    return slice(hh * HD, hh * HD + HD)


def v_slot(head):
    return head + 4 if head < 4 else head - 4


def head_tops(pair, hh):
    maxima = [("max", pair, hh, qb, kh) for qb in range(TB) for kh in range(2)]
    return maxima[:10] + [("shift", pair, hh, 0)] + maxima[10:] + [("shift", pair, hh, 1)]


def top_uses(step, u, last=False):
    w, hh = u % 8, u // 8
    if last and step == 3 and hh == 1:
        return []
    done = sum(TOPS_PER_W[:w])
    return head_tops(*((step, 1) if hh == 0 else ((step + 1) % 4, 0)))[done:done + TOPS_PER_W[w]]


TOPS_SINCE_SHIFT = (7, sum(TOPS_PER_W[:4]))


SIDE = [
    {0: "qk", 1: ("ot", 2, 0), 2: "qk", 3: ("ot", 2, 1), 4: "qk", 5: "qk", 6: ("ot", 3, 0),
     7: ("ot", 3, 1), 8: "out", 10: "out", 12: "out", 13: "out", 14: "out", 15: "out"},
    {0: "qk", 1: "xt", 2: "qk", 3: "xt", 4: "qk", 5: "xt", 6: "qk", 7: "xt", 8: "xt", 9: "xt", 10: "xt",
     11: "xt", 13: "out", 14: "out"},
    {0: ("ot", 0, 0), 1: ("ot", 0, 1), 2: "mean", 3: "qk", 4: "var", 5: "qk", 6: "qk", 7: "qk", 12: "v",
     13: "v", 14: "v"},
    {0: "qk", 1: ("ot", 1, 0), 2: "qk", 3: ("ot", 1, 1), 4: "qk", 5: "qk", 8: "v", 10: "v", 12: "v",
     13: "v", 14: "v"},
]
TOPS_AHEAD = [[1, 0], [0, 0]]
TOP_PLACES = [[(1, 2, 3), (2, 2, 3)], [(0, 1, 3), (1, 1, 3)]]
PLACE_AT = 10
SPLIT = ("qk", "v", "out")


def side_uses(step, u, first=False, last=False):
    kind = SIDE[step].get(u)
    if kind is None:
        return []
    if kind[0] == "ot":
        return [] if first and step == 0 else [kind]
    n = sum(k == kind for at, k in SIDE[step].items() if at < u)
    if kind == "qk":
        return [] if last and step == 3 else [("qk", (step + 1) % 4, "qk"[n % 2], n // 2)]
    if kind == "out":
        return [] if first else [("out", n + (list(SIDE[0].values()).count("out") if step == 1 else 0))]
    if last:
        return []
    if kind == "v":
        n += list(SIDE[2].values()).count("v") if step == 3 else 0
    return [(kind, n)]


def side_before(step, u, first=False, last=False):
    if u > 0:
        return side_uses(step, u - 1, first, last)
    return side_uses(step - 1, 15, first, last) if step > 0 else []


def follows_split(step, u, first=False, last=False):
    return any(use[0] in SPLIT for use in side_before(step, u, first, last))


def image_of(use, b, step):
    if use[0] in ("xt", "mean", "var", "v") or (use[0] == "qk" and step == 3):
        return b + 1
    if use[0] == "out" or (use[0] == "ot" and step == 0):
        return b - 1
    return b


def image_before(use, b, step, u):
    return image_of(use, b, step if u > 0 else step - 1)


SIDE_PROLOGUE = ([("xt", t) for t in range(TB)] + [("mean", 0), ("var", 0)]
                 + [("qk", 0, "qk"[i % 2], i // 2) for i in range(4)] + [("v", t) for t in range(TB)])
PROLOGUE = (SIDE_PROLOGUE[:-TB]
            + [use for t in range(TB) for use in [("v", t)] + head_tops(0, 0)[9 * t // 4:9 * (t + 1) // 4]])
EPILOGUE = [("ot", pair, half) for pair in (2, 3) for half in (0, 1)] + [("out", t) for t in range(TB)]
IMAGE_USES = [x for s in range(4) for u in range(16) for x in side_uses(s, u)]
HI_PARTS = ("qk", "v", "ot")


class Count:
    PER_IMAGE = {"side": len(IMAGE_USES), "hi": sum(x[0] in HI_PARTS for x in IMAGE_USES),
                 "top": HEADS * 18, "shifts": 2 * HEADS}

    def __init__(self, side=0, hi=0, top=0, shifts=0, mark=None):
        self.side, self.hi, self.top, self.shifts, self.top_bank = side, hi, top, shifts, 0
        self.mark = dict(mark or {"qk": 0, "v": 0, "ot": 0})

    def passed(self, use):
        if use[0] in ("max", "shift"):
            self.top = self.top + 1
            self.top_bank = 1 - self.top_bank
            if use[0] == "shift":
                self.shifts = self.shifts + 1
            return
        self.side = self.side + 1
        self.hi = self.hi + (use[0] in HI_PARTS)
        if use[0] in self.mark:
            self.mark[use[0]] = self.side

    def later(self, images):
        n = {name: images * per for name, per in self.PER_IMAGE.items()}
        then = Count(self.side + n["side"], self.hi + n["hi"], self.top + n["top"], self.shifts + n["shifts"],
                     {kind: at + n["side"] for kind, at in self.mark.items()})
        then.top_bank = self.top_bank
        return then


def wait(eng, sem, count):
    if not isinstance(count, int) or count > 0:
        eng.wait_ge(sem, count)


def conv_attention(nc, x, gamma, beta, w_qkv, w_out, b_out, out):
    x_blocks = x.rearrange("b h w c -> (b h w) c").rearrange("(n p) c -> n p c", p=P)
    out_blocks = out.rearrange("b h w c -> (b h w) c").rearrange("(n p) c -> n p c", p=P)

    ctx = ExitStack()
    with ctx:
        def sb(name, shape, dt):
            return ctx.enter_context(nc.sbuf_tensor(name, shape, dt))

        def ps(name, shape, dt):
            return ctx.enter_context(nc.psum_tensor(name, shape, dt))

        def sem(name):
            return ctx.enter_context(nc.semaphore(name))

        ident32 = sb("ident32", [P, P], F32)
        ident16 = sb("ident16", [P, P], F16)
        group_mean = sb("group_mean", [P, P], F32)
        gam = sb("gam", [P, CC], F32)
        bet = sb("bet", [P, CC], F32)
        bias = sb("bias", [P, CH], F32)
        wq = sb("wq", [P, 2, CC, 3 * CH], F16)
        wo = sb("wo", [P, 2, CC, CH], F16)
        red = sb("red", [P, 8], F32)
        top = sb("top", [P, 8], F32)
        pw = sb("pw", [P, 8], F32)
        sc = sb("sc", [P, 8], F32)
        inv = sb("inv", [P, 8], F32)
        tot = sb("tot", [P, 8], F32)
        cns = sb("cns", [P, 4], F32)
        absg = sb("absg", [P, CC], F32)
        absb = sb("absb", [P, CC], F32)
        bound = sb("bound", [P, CC], F32)
        bound16 = sb("bound16", [P, CC], F16)
        work = sb("work", [P, 6 * TOK], F32)
        xT = work[:, 0:4 * TOK].rearrange("p (c n) -> p c n", c=CC)
        z = work[:, 4 * TOK:5 * TOK].rearrange("p (i n) -> p i n", i=2)
        th = work[:, 5 * TOK:6 * TOK].rearrange("p (i n) -> p i n", i=2)
        x_in = z
        st = sb("st", [P, CC, 12], F32)
        mv = sb("mv", [P, CC, 2], F32)
        gn = sb("gn", [P, 16, CC], F32)
        gmean, dev, dev2, vd, veps, half_v, three_halves, half_bits, root, a_c, ma_c, b_c, ah, bh, az, bz = (
            gn[:, i, :] for i in range(16))
        nt = sb("nt", [P, 2, CC], F32)
        xn = sb("xn", [P, 2, CC, TOK], F16)
        QK_hi = sb("QK_hi", [P, 2, 2, TOK], F16)
        QK_lo = sb("QK_lo", [P, 2, TOK], F16)
        K1 = sb("K1", [P, 4, TOK], F16)
        K2 = sb("K2", [P, 4, TOK], F16)
        Q1 = sb("Q1", [P, 4, TOK], F16)
        Q2 = sb("Q2", [P, 4, TOK], F16)
        V = sb("V", [P, TB, 12, VW], F16)
        mx = sb("mx", [P, 2, TB, 2], F32)
        mx8 = sb("mx8", [P, TB], F32)
        ms = sb("ms", [P, 2, TB], F16)
        P32 = sb("P32", [P, 2, 2 * HALF], F32)
        Ph = sb("Ph", [P, 4, 2 * HALF], F16)
        Pl = sb("Pl", [P, 4, 2 * HALF], F16)
        pv_sum = sb("pv_sum", [P, 2, 4, LO + HD], F32)
        den = sb("den", [P, 2, 4], F32)
        O32 = sb("O32", [P, 2, TB, P], F32)
        OT = sb("OT", [P, 2, CC, TOK], F16)
        res = sb("res", [P, 4, CH], F32)

        w_stage = V[:, :, :, :].rearrange("p t h c -> p (t h c)")[:, 0:2 * CC * 3 * CH].bitcast(F32).rearrange(
            "p (c n) -> p c n", c=CC)
        wo_stage = P32[:, :, :].rearrange("p a b -> p (a b)").rearrange("p (c n) -> p c n", c=CC)
        w_abs = xn[:, :, :, :].rearrange("p a c n -> p (a c n)")[:, 0:CC * 3 * CH].rearrange(
            "p (c n) -> p c n", c=CC)

        ST = ps("ST", [P, 2, 2 * HALF], F32)
        PV = ps("PV", [P, 512], F32)
        SD = ps("SD", [P, 512], F32)
        TP = ps("TP", [P, 2, 512], F32)

        bound_psum = ST[:, :, :].rearrange("p a (b n) -> p (a b) n", n=512)

        w_loaded = sem("w_loaded")
        const_ready = sem("const_ready")
        maxima_in = sem("maxima_in")
        maxima_out = sem("maxima_out")
        setup_step = sem("setup_step")
        wq_ready = sem("wq_ready")
        w_abs_ready = sem("w_abs_ready")
        bound_out = sem("bound_out")
        setup_done = sem("setup_done")
        x_loaded = [sem(f"x_loaded{i}") for i in range(2)]
        res_loaded = [sem(f"res_loaded{i}") for i in range(4)]
        res_biased = sem("res_biased")
        stored = [sem(f"stored{i}") for i in range(4)]
        side_filled = sem("side_filled")
        placed = [sem(f"placed{i}") for i in range(2)]
        side_hi = sem("side_hi")
        side_drained = sem("side_drained")
        top_filled = sem("top_filled")
        top_drained = sem("top_drained")
        bn_done = sem("bn_done")
        chan_stats = sem("chan_stats")
        dve_step = sem("dve_step")
        dev_ready = sem("dev_ready")
        guess_ready = sem("guess_ready")
        newton_step = sem("newton_step")
        coef_ready = sem("coef_ready")
        silu_ready = sem("silu_ready")
        xn_f32 = sem("xn_f32")
        xn_hi = sem("xn_hi")
        xn_lo = sem("xn_lo")
        v_moved = sem("v_moved")
        mx8_ready = sem("mx8_ready")
        shift_ready = sem("shift_ready")
        scores_ready = sem("scores_ready")
        exp_done = sem("exp_done")
        lo_dve = sem("lo_dve")
        lo_pool = sem("lo_pool")
        pv_done = sem("pv_done")
        pv_out = sem("pv_out")
        den_ready = sem("den_ready")
        o_normed = sem("o_normed")

        def wait_placed(eng, pairs):
            for hh in range(2):
                wait(eng, placed[hh], PLACED * pairs)

        block = ctx.enter_context(nc.Block())

        @block.sync
        def _(sp):
            sp.dma_start(w_stage, w_qkv.rearrange("(c p) n -> p c n", p=P)).then_inc(w_loaded, 16)
            sp.dma_start(wo_stage, w_out.rearrange("(c p) n -> p c n", p=P)).then_inc(w_loaded, 16)
            sp.dma_start(gam[:], gamma.rearrange("(c p) -> p c", p=P), allow_slow_non_contiguous=True).then_inc(w_loaded, 16)
            sp.dma_start(bet[:], beta.rearrange("(c p) -> p c", p=P), allow_slow_non_contiguous=True).then_inc(w_loaded, 16)
            sp.dma_start(bias[:], b_out.rearrange("(o c) -> o c", o=1).to_broadcast([P, CH])
                         ).then_inc(w_loaded, 16)

            def load_x(image, t, filled):
                src = x_blocks[bass.ds(sp.snap(image * TB + t), 1)].rearrange("o p c -> p (o c)")
                wait(sp, side_filled, filled)
                sp.dma_start(x_in[:, t % 2, :], src).then_inc(x_loaded[t % 2], 16)

            def load_res(image, t):
                src = x_blocks[bass.ds(sp.snap(image * TB + t), 1)].rearrange("o p c -> p (o c)")
                wait(sp, stored[t % 4], 32 * image + 16 * (t // 4))
                sp.dma_start(res[:, t % 4, :], src).then_inc(res_loaded[t % 4], 16)

            def store(image, t, drained):
                dst = out_blocks[bass.ds(sp.snap(image * TB + t), 1)].rearrange("o p c -> p (o c)")
                wait(sp, side_drained, drained)
                sp.dma_start(dst, res[:, t % 4, :]).then_inc(stored[t % 4], 16)

            def place(pair, cnt):
                sp.wait_ge(side_drained, cnt.mark["qk"])
                for hh in range(2):
                    r, other, slot = rows_of(hh), rows_of(1 - hh), head_slot(pair, hh)
                    q_hi, k_hi = QK_hi[r, pair % 2, 0, :], QK_hi[r, pair % 2, 1, :]
                    for dst, src in ((Q1[r, slot, :], q_hi), (K1[r, slot, :], k_hi),
                                     (Q1[other, slot, :], q_hi), (K1[other, slot, :], QK_lo[r, 1, :]),
                                     (Q2[r, slot, :], QK_lo[r, 0, :]), (K2[r, slot, :], k_hi)):
                        sp.dma_start(dst, src).then_inc(placed[hh], 16)

            def step(b, s, cnt, first=False, last=False):
                filled = []
                if s == 2:
                    for t in range(4):
                        load_res(b, t)
                for u in range(16):
                    for use in side_uses(s, u, first, last):
                        cnt.passed(use)
                        if use[0] == "xt":
                            filled.append(cnt.side)
                            if use[1] < TB - 2:
                                load_x(b + 1, use[1] + 2, filled[use[1]])
                        if use[0] == "out":
                            store(b - 1, use[1], cnt.side)
                            if use[1] < 4:
                                load_res(b - 1, use[1] + 4)
                    if s == 0 and u == 9 and not last:
                        load_x(b + 1, 0, cnt.side)
                        load_x(b + 1, 1, cnt.side)
                    if u == PLACE_AT and not (last and s == 3):
                        place((s + 1) % 4, cnt)

            cnt = Count()
            for use in SIDE_PROLOGUE:
                cnt.passed(use)
                if use[0] == "xt":
                    load_x(0, use[1], use[1] - 1)
                if use == ("qk", 0, "k", 1):
                    place(0, cnt)
            step(0, 0, cnt, first=True)
            step(0, 1, cnt, first=True)
            with sp.Fori(0, B - 2) as b:
                now = cnt.later(b)
                step(b, 2, now)
                step(b, 3, now)
                step(b + 1, 0, now)
                step(b + 1, 1, now)
            now = cnt.later(B - 2)
            step(B - 2, 2, now)
            step(B - 2, 3, now)
            for s in range(4):
                step(B - 1, s, now, last=True)
            for use in EPILOGUE:
                now.passed(use)
                if use[0] == "out":
                    store(B - 1, use[1], now.side)
                    if use[1] < 4:
                        load_res(B - 1, use[1] + 4)
            for t in range(4):
                sp.wait_ge(stored[t], 32 * B)

        @block.gpsimd
        def _(pool):
            nc.gpsimd.memset(ident32[:], 0.0).then_inc(const_ready, 1)
            nc.gpsimd.memset(group_mean[:], 1.0 / GROUP).then_inc(const_ready, 1)
            pool.wait_ge(const_ready, 2)
            nc.gpsimd.affine_select(out=ident32[:], in_=ident32[:], compare_op=ALU.not_equal, fill=1.0, base=0,
                                    pattern=[[-1, P]], channel_multiplier=1).then_inc(const_ready, 1)
            grouped = group_mean[:].rearrange("p (g c) -> p g c", c=GROUP)
            nc.gpsimd.affine_select(out=grouped, in_=grouped, compare_op=ALU.is_ge, fill=0.0, base=0,
                                    pattern=[[-GROUP, P // GROUP], [0, GROUP]], channel_multiplier=1
                                    ).then_inc(const_ready, 1)
            pool.wait_ge(const_ready, 4)
            nc.gpsimd.affine_select(out=grouped, in_=grouped, compare_op=ALU.is_ge, fill=0.0, base=GROUP - 1,
                                    pattern=[[GROUP, P // GROUP], [0, GROUP]], channel_multiplier=-1
                                    ).then_inc(const_ready, 1)
            pool.wait_ge(maxima_in, 1)
            nc.gpsimd.partition_all_reduce(top[:, 0:3], red[:, 0:3], P, bass.bass_isa.ReduceOp.max
                                           ).then_inc(maxima_out, 1)
            pool.wait_ge(setup_done, 1)

            def newton(image):
                n = 4 * NEWTON * image
                pool.wait_ge(guess_ready, image + 1)
                for i in range(0, 4 * NEWTON, 4):
                    nc.gpsimd.tensor_tensor(nt[:, 0, :], root, root, ALU.mult).then_inc(newton_step, 1)
                    pool.wait_ge(newton_step, n + i + 1)
                    nc.gpsimd.tensor_tensor(nt[:, 1, :], nt[:, 0, :], half_v, ALU.mult).then_inc(newton_step, 1)
                    pool.wait_ge(newton_step, n + i + 2)
                    nc.gpsimd.tensor_tensor(nt[:, 0, :], three_halves, nt[:, 1, :], ALU.subtract
                                            ).then_inc(newton_step, 1)
                    pool.wait_ge(newton_step, n + i + 3)
                    nc.gpsimd.tensor_tensor(root, root, nt[:, 0, :], ALU.mult).then_inc(newton_step, 1)
                    pool.wait_ge(newton_step, n + i + 4)

            def low_xn(image, i):
                c, tokens = i % CC, bass.ts(i // CC, HALF)
                pool.wait_ge(xn_hi, PIECES * image + i + 1)
                nc.gpsimd.tensor_tensor(xn[:, 1, c, tokens], xT[:, c, tokens], xn[:, 0, c, tokens],
                                        ALU.subtract).then_inc(xn_lo, 1)

            def add_bias(image, t):
                pool.wait_ge(res_loaded[t % 4], 32 * image + 16 * (t // 4) + 16)
                nc.gpsimd.tensor_tensor(res[:, t % 4, :], res[:, t % 4, :], bias[:], ALU.add
                                        ).then_inc(res_biased, 1)

            def low_probs(b, v):
                pool.wait_ge(exp_done, UNITS * b + v + 1)
                wait(pool, pv_done, UNITS * b + v - 3)
                nc.gpsimd.tensor_tensor(Pl[:, v % 4, :], P32[:, v % 2, :], Ph[:, v % 4, :], ALU.subtract
                                        ).then_inc(lo_pool, 1)

            def normalise(b, half):
                pool.wait_ge(den_ready, 16 * b + half + 1)
                pair, hh, q = half // 4 % 4, half // 2 % 2, half % 2
                nc.gpsimd.tensor_tensor(O32[:, pair % 2, 4 * q:4 * q + 4, rows_of(hh)],
                                        pv_sum[:, half % 2, :, 0:HD],
                                        den[:, half % 2, :].unsqueeze(2).to_broadcast([P, 4, HD]), ALU.mult
                                        ).then_inc(o_normed, 1)

            LATE_BIAS = {(0, 12): 4, (0, 14): 5, (0, 15): 6, (1, 2): 7}

            def step(b, s, first=False, last=False):
                for u in range(16):
                    v = 16 * s + u
                    if v % 2 == 0 and not (first and v == 0):
                        low_probs(b, v - 1)
                    if v % 4 == 1 and not (first and v == 1):
                        normalise(b, v // 4 - 1)
                    if s == 2 and u == 5 and not last:
                        newton(b + 1)
                    if s == 2 and 8 <= u and not last:
                        low_xn(b + 1, u - 8)
                    if s == 3 and u < 4:
                        add_bias(b, u)
                    if (s, u) in LATE_BIAS and not first:
                        add_bias(b - 1, LATE_BIAS[s, u])

            newton(0)
            for i in range(PIECES):
                low_xn(0, i)
            step(0, 0, first=True)
            step(0, 1, first=True)
            with pool.Fori(0, B - 2) as b:
                step(b, 2)
                step(b, 3)
                step(b + 1, 0)
                step(b + 1, 1)
            step(B - 2, 2)
            step(B - 2, 3)
            for s in range(4):
                step(B - 1, s, last=True)
            low_probs(B - 1, UNITS - 1)
            normalise(B - 1, 15)
            for t in range(4, 8):
                add_bias(B - 1, t)

        @block.scalar
        def _(act):
            def side(use, image, cnt):
                if use[0] in HI_PARTS or use[0] == "xt":
                    act.wait_ge(side_filled, cnt.side + 1)
                if use[0] == "qk":
                    _, pair, which, half = use
                    wait_placed(act, 4 * image + pair - 1)
                    i, col = (0, Q_SCALE) if which == "q" else (1, K_SCALE)
                    nc.scalar.activation(QK_hi[:, pair % 2, i, bass.ts(half, HALF)], SD[:], ACT.Identity,
                                         scale=sc[:, col:col + 1]).then_inc(side_hi, 1)
                if use[0] == "v":
                    wait(act, v_moved, image)
                    nc.scalar.activation(V[:, use[1], 4:12, 0:HD],
                                         SD[:].rearrange("p (h d) -> p h d", d=HD), ACT.Identity,
                                         scale=sc[:, V_SCALE:V_SCALE + 1]).then_inc(side_hi, 1)
                if use[0] == "xt":
                    wait(act, xn_lo, PIECES * image)
                    wait(act, xn_hi, PIECES * image)
                    nc.scalar.activation(xT[:, :, bass.ts(use[1], P)], SD[:].rearrange("p (c n) -> p c n", c=CC),
                                         ACT.Copy).then_inc(side_drained, 1)
                if use[0] == "ot":
                    _, pair, half = use
                    nc.scalar.activation(OT[:, 0, pair, bass.ts(half, HALF)], SD[:], ACT.Copy
                                         ).then_inc(side_hi, 1)
                cnt.passed(use)

            def silu_parts(image, i):
                c, tokens = i % CC, bass.ts(i // CC, HALF)
                act.wait_ge(coef_ready, image + 1)
                wait(act, xn_f32, PIECES * image + i - 1)
                nc.scalar.activation(z[:, i % 2], xT[:, c, tokens], ACT.Identity, scale=az[:, c:c + 1],
                                     bias=bz[:, c:c + 1])
                nc.scalar.activation(th[:, i % 2], xT[:, c, tokens], ACT.Tanh, scale=ah[:, c:c + 1],
                                     bias=bh[:, c:c + 1]).then_inc(silu_ready, 1)

            def exponentials(b, v):
                act.wait_ge(scores_ready, UNITS * b + v + 1)
                if v % 2 == 0:
                    wait(act, lo_dve, 32 * b + v // 2)
                else:
                    wait(act, lo_pool, 32 * b + v // 2)
                nc.scalar.activation(P32[:, v % 2, :], ST[:, v % 2, :], ACT.Exp, scale=cns[:, 0:1])
                wait(act, pv_done, UNITS * b + v - 3)
                nc.scalar.activation(Ph[:, v % 4, :], ST[:, v % 2, :], ACT.Exp, scale=cns[:, 0:1]
                                     ).then_inc(exp_done, 1)

            def sums_out(b, half):
                act.wait_ge(pv_done, UNITS * b + 4 * half + 4)
                wait(act, o_normed, 16 * b + half - 1)
                nc.scalar.activation(pv_sum[:, half % 2].rearrange("p q c -> p (q c)")[:, 0:PV_COLS],
                                     PV[:, 0:PV_COLS], ACT.Copy).then_inc(pv_out, 1)

            def step(b, s, cnt, first=False, last=False):
                for u in range(16):
                    v = 16 * s + u
                    for use in side_before(s, u, first, last):
                        side(use, image_before(use, b, s, u), cnt)
                    exponentials(b, v)
                    if v % 4 == 1 and not (first and v == 1):
                        sums_out(b, v // 4 - 1)
                    if s == 2 and 7 <= u < 15 and not last:
                        silu_parts(b + 1, u - 7)

            cnt = Count()
            for use in PROLOGUE[:TB]:
                side(use, 0, cnt)
            act.wait_ge(wq_ready, 1)
            nc.scalar.activation(w_abs, wq[:, 0], ACT.Abs).then_inc(w_abs_ready, 1)
            act.wait_ge(setup_done, 1)
            for use in SIDE_PROLOGUE[TB:]:
                side(use, 0, cnt)
                if use[0] == "var":
                    for i in range(PIECES):
                        silu_parts(0, i)
            step(0, 0, cnt, first=True)
            step(0, 1, cnt, first=True)
            with act.Fori(0, B - 2) as b:
                now = cnt.later(b)
                step(b, 2, now)
                step(b, 3, now)
                step(b + 1, 0, now)
                step(b + 1, 1, now)
            now = cnt.later(B - 2)
            step(B - 2, 2, now)
            step(B - 2, 3, now)
            for s in range(4):
                step(B - 1, s, now, last=True)
            sums_out(B - 1, 15)
            for use in EPILOGUE:
                side(use, B - 1, now)

        @block.vector
        def _(dve):
            steps = [0]

            def then(ins):
                steps[0] += 1
                ins.then_inc(setup_step, 1)
                dve.wait_ge(setup_step, steps[0])

            def scale_of(dst, inverse, size):
                n = size.shape[1]
                then(nc.vector.tensor_scalar(size, size, 1e-30, None, ALU.max))
                then(nc.vector.tensor_scalar(pw[:, 0:n].bitcast(I32), size.bitcast(I32), EXPONENT, None,
                                             ALU.bitwise_and))
                then(nc.vector.tensor_scalar(inverse, pw[:, 0:n], 1.0 / TOP, None, ALU.mult))
                then(nc.vector.reciprocal(dst, inverse))

            def side(use, image, cnt):
                kind = use[0]
                if kind == "xt":
                    cnt.passed(use)
                    return
                dve.wait_ge(side_filled, cnt.side + 1)
                if kind in HI_PARTS:
                    dve.wait_ge(side_hi, cnt.hi + 1)
                if kind == "qk":
                    _, pair, which, half = use
                    cols = bass.ts(half, HALF)
                    wait_placed(dve, 4 * image + pair)
                    i, col = (0, Q_SCALE) if which == "q" else (1, K_SCALE)
                    nc.vector.scalar_tensor_tensor(out=QK_lo[:, i, cols], in0=SD[:], scalar=sc[:, col:col + 1],
                                                   in1=QK_hi[:, pair % 2, i, cols], op0=ALU.mult,
                                                   op1=ALU.subtract).then_inc(side_drained, 1)
                if kind == "v":
                    wait(dve, v_moved, image)
                    nc.vector.scalar_tensor_tensor(
                        out=V[:, use[1], 4:12, LO:LO + HD], in0=SD[:].rearrange("p (h d) -> p h d", d=HD),
                        scalar=sc[:, V_SCALE:V_SCALE + 1], in1=V[:, use[1], 4:12, 0:HD],
                        op0=ALU.mult, op1=ALU.subtract).then_inc(side_drained, 1)
                if kind == "ot":
                    _, pair, half = use
                    cols = bass.ts(half, HALF)
                    nc.vector.tensor_tensor(OT[:, 1, pair, cols], SD[:], OT[:, 0, pair, cols],
                                            ALU.subtract).then_inc(side_drained, 1)
                if kind == "out":
                    dve.wait_ge(res_biased, TB * image + use[1] + 1)
                    nc.vector.scalar_tensor_tensor(out=res[:, use[1] % 4, :], in0=SD[:],
                                                   scalar=cns[:, 1:2], in1=res[:, use[1] % 4, :],
                                                   op0=ALU.mult, op1=ALU.add).then_inc(side_drained, 1)
                if kind == "mean":
                    n = DVE_STEPS * image
                    nc.vector.tensor_copy(gmean, SD[:, 0:CC]).then_inc(side_drained, 1)
                    dve.wait_ge(side_drained, cnt.side + 1)
                    nc.vector.tensor_tensor(dev, mv[:, :, 0], gmean, ALU.subtract).then_inc(dve_step, 1)
                    dve.wait_ge(dve_step, n + 1)
                    nc.vector.tensor_tensor(dev2, dev, dev, ALU.mult).then_inc(dve_step, 1)
                    dve.wait_ge(dve_step, n + 2)
                    nc.vector.tensor_tensor(vd, dev2, mv[:, :, 1], ALU.add).then_inc(dev_ready, 1)
                if kind == "var":
                    n = DVE_STEPS * image + 2
                    nc.vector.tensor_scalar(veps, SD[:, 0:CC], EPS, None, ALU.add
                                            ).then_inc(side_drained, 1)
                    dve.wait_ge(side_drained, cnt.side + 1)
                    nc.vector.tensor_scalar(half_v, veps, 0.5, None, ALU.mult)
                    nc.vector.tensor_scalar(half_bits.bitcast(I32), veps.bitcast(I32), 1, None,
                                            ALU.logical_shift_right).then_inc(dve_step, 1)
                    dve.wait_ge(dve_step, n + 1)
                    nc.vector.tensor_scalar(root.bitcast(I32), half_bits.bitcast(I32), -1.0, RSQRT_GUESS,
                                            ALU.mult, ALU.add).then_inc(guess_ready, 1)
                cnt.passed(use)

            def shifts(hh, half, cnt):
                blocks = slice(4 * half, 4 * half + 4)
                dve.wait_ge(top_drained, cnt.top)
                nc.vector.tensor_reduce(mx8[:, blocks], mx[:, hh, blocks], AX.X, ALU.max).then_inc(mx8_ready, 1)
                dve.wait_ge(mx8_ready, cnt.shifts + 1)
                nc.vector.tensor_scalar(ms[:, hh, blocks], mx8[:, blocks], cns[:, 3:4], -1.0 / (HD * ROWC),
                                        ALU.subtract, ALU.mult).then_inc(shift_ready, 1)

            def top_use(use, cnt):
                dve.wait_ge(top_filled, cnt.top + 1)
                if use[0] == "max":
                    _, pair, hh, qb, kh = use
                    nc.vector.reduce_max(mx[:, hh, qb, kh:kh + 1], TP[:, cnt.top_bank], AX.X
                                         ).then_inc(top_drained, 1)
                else:
                    _, pair, hh, half = use
                    r = rows_of(1 - hh)
                    nc.vector.tensor_copy(Q2[r, head_slot(pair, hh), bass.ts(half, HALF)], TP[r, cnt.top_bank]
                                          ).then_inc(top_drained, 1)
                cnt.passed(use)
                if use[0] == "max" and use[3:] in ((3, 1), (7, 1)):
                    shifts(use[2], use[3] // 4, cnt)

            def channel_stats(image, i, cnt):
                dve.wait_ge(side_drained, cnt.side)
                c, half = i // 2, i % 2
                stats = nc.vector.bn_stats(st[:, c, 6 * half:6 * half + 6], xT[:, c, bass.ts(half, HALF)])
                if i == 7:
                    stats.then_inc(bn_done, 1)

            def aggregate(image):
                for c in range(CC):
                    aggr = nc.vector.bn_aggr(mv[:, c, :], st[:, c, :])
                aggr.then_inc(chan_stats, 1)
                dve.wait_ge(chan_stats, image + 1)

            def coefficients(image):
                n = DVE_STEPS * image + 3
                dve.wait_ge(newton_step, 4 * NEWTON * (image + 1))
                nc.vector.tensor_tensor(a_c, gam[:], root, ALU.mult).then_inc(dve_step, 1)
                dve.wait_ge(dve_step, n + 1)
                nc.vector.tensor_tensor(ma_c, gmean, a_c, ALU.mult).then_inc(dve_step, 1)
                dve.wait_ge(dve_step, n + 2)
                nc.vector.tensor_tensor(b_c, bet[:], ma_c, ALU.subtract).then_inc(dve_step, 1)
                dve.wait_ge(dve_step, n + 3)
                nc.vector.tensor_scalar(ah, a_c, 0.5, None, ALU.mult)
                nc.vector.tensor_scalar(bh, b_c, 0.5, None, ALU.mult).then_inc(dve_step, 1)
                dve.wait_ge(dve_step, n + 4)
                nc.vector.tensor_scalar(az, ah, sc[:, 2:3], None, ALU.mult)
                nc.vector.tensor_scalar(bz, bh, sc[:, 2:3], None, ALU.mult).then_inc(coef_ready, 1)

            def silu(image, i):
                c, tokens = i % CC, bass.ts(i // CC, HALF)
                dve.wait_ge(silu_ready, PIECES * image + i + 1)
                nc.vector.scalar_tensor_tensor(out=xT[:, c, tokens], in0=th[:, i % 2], scalar=1.0, in1=z[:, i % 2],
                                               op0=ALU.add, op1=ALU.mult).then_inc(xn_f32, 1)
                dve.wait_ge(xn_f32, PIECES * image + i + 1)
                nc.vector.tensor_copy(xn[:, 0, c, tokens], xT[:, c, tokens]).then_inc(xn_hi, 1)

            def low_probs(b, v):
                dve.wait_ge(exp_done, UNITS * b + v + 1)
                wait(dve, pv_done, UNITS * b + v - 3)
                nc.vector.tensor_tensor(Pl[:, v % 4, :], P32[:, v % 2, :], Ph[:, v % 4, :], ALU.subtract
                                        ).then_inc(lo_dve, 1)

            def sums(b, half):
                dve.wait_ge(pv_out, 16 * b + half + 1)
                nc.vector.reciprocal(den[:, half % 2, :], pv_sum[:, half % 2, :, HD])
                nc.vector.tensor_tensor(pv_sum[:, half % 2, 0:3, 0:HD], pv_sum[:, half % 2, 0:3, 0:HD],
                                        pv_sum[:, half % 2, 0:3, LO:LO + HD], ALU.add).then_inc(den_ready, 1)

            def move_v(b, cnt):
                wait(dve, pv_done, UNITS * b)
                dve.wait_ge(side_drained, cnt.side)
                nc.vector.tensor_copy(V[:, :, 0:4, :], V[:, :, 8:12, :]).then_inc(v_moved, 1)

            def step(b, s, cnt, first=False, last=False):
                for u in range(16):
                    v = 16 * s + u
                    for use in side_before(s, u, first, last):
                        side(use, image_before(use, b, s, u), cnt)
                    tops = top_uses(s, u, last)
                    late = follows_split(s, u, first, last)
                    ahead = TOPS_AHEAD[u % 8 == 7][late]
                    for use in tops[:ahead]:
                        top_use(use, cnt)
                    if v % 2 == 1:
                        low_probs(b, v - 1)
                    for use in tops[ahead:]:
                        top_use(use, cnt)
                    if v % 4 == 1 and not (first and v == 1):
                        sums(b, v // 4 - 1)
                    if s == 0 and u == 7:
                        move_v(b, cnt)
                    if s == 1 and u >= 12 and not last:
                        channel_stats(b + 1, 2 * u - 24, cnt)
                        channel_stats(b + 1, 2 * u - 23, cnt)
                    if s == 2 and not last:
                        if u == 1:
                            aggregate(b + 1)
                        if u == 6:
                            coefficients(b + 1)
                        if u >= 8:
                            silu(b + 1, u - 8)

            nc.vector.memset(K2[:], ROWC)
            nc.vector.memset(three_halves, 1.5)
            dve.wait_ge(const_ready, 5)
            nc.vector.tensor_copy(ident16[:], ident32[:])
            dve.wait_ge(w_loaded, 16 * 5)
            then(nc.vector.tensor_reduce(red[:, 0:1], w_stage, AX.XY, ALU.max, apply_absolute_value=True))
            then(nc.vector.tensor_reduce(red[:, 1:2], wo_stage, AX.XY, ALU.max, apply_absolute_value=True))
            then(nc.vector.scalar_tensor_tensor(out=absg[:], in0=gam[:], scalar=-1.0, in1=gam[:],
                                                op0=ALU.mult, op1=ALU.max))
            then(nc.vector.scalar_tensor_tensor(out=absb[:], in0=bet[:], scalar=-1.0, in1=bet[:],
                                                op0=ALU.mult, op1=ALU.max))
            then(nc.vector.scalar_tensor_tensor(out=bound[:], in0=absg[:], scalar=NORMED_MAX, in1=absb[:],
                                                op0=ALU.mult, op1=ALU.add))
            nc.vector.tensor_reduce(red[:, 2:3], bound[:], AX.X, ALU.max).then_inc(maxima_in, 1)
            dve.wait_ge(maxima_out, 1)
            scale_of(sc[:, 0:3], inv[:, 0:3], top[:, 0:3])
            nc.vector.tensor_scalar(bound16[:], bound[:], sc[:, 2:3], None, ALU.mult)
            nc.vector.tensor_scalar(wq[:, 0], w_stage, sc[:, 0:1], None, ALU.mult).then_inc(wq_ready, 1)
            dve.wait_ge(wq_ready, 1)
            then(nc.vector.scalar_tensor_tensor(out=wq[:, 1], in0=w_stage, scalar=sc[:, 0:1], in1=wq[:, 0],
                                                op0=ALU.mult, op1=ALU.subtract))
            then(nc.vector.tensor_scalar(wo[:, 0], wo_stage, sc[:, 1:2], None, ALU.mult))
            then(nc.vector.scalar_tensor_tensor(out=wo[:, 1], in0=wo_stage, scalar=sc[:, 1:2], in1=wo[:, 0],
                                                op0=ALU.mult, op1=ALU.subtract))
            nc.vector.memset(V[:, :, :, HD:LO], 1.0)
            nc.vector.memset(V[:, :, :, VW - 1:VW], 0.0)
            cnt = Count()
            for use in PROLOGUE[:TB]:
                side(use, 0, cnt)
            for i in range(8):
                channel_stats(0, i, cnt)
            dve.wait_ge(bn_done, 1)
            aggregate(0)
            dve.wait_ge(bound_out, 1)
            for i in range(3):
                then(nc.vector.tensor_reduce(top[:, 3 + i:4 + i], bound_psum[:, i, :], AX.X, ALU.max))
            scale_of(sc[:, 3:6], inv[:, 3:6], top[:, 3:6])
            then(nc.vector.tensor_scalar(tot[:, 0:3], inv[:, 3:6], inv[:, 0:1], inv[:, 2:3], ALU.mult, ALU.mult))
            then(nc.vector.tensor_scalar(cns[:, 0:1], tot[:, 0:1], tot[:, 1:2], HD ** -0.5, ALU.mult, ALU.mult))
            then(nc.vector.tensor_scalar(cns[:, 1:2], tot[:, 2:3], inv[:, 1:2], None, ALU.mult))
            then(nc.vector.reciprocal(cns[:, 2:3], cns[:, 0:1]))
            nc.vector.tensor_scalar(cns[:, 3:4], cns[:, 2:3], SHIFT_UP, None, ALU.mult).then_inc(setup_done, 1)
            dve.wait_ge(setup_done, 1)


            for use in PROLOGUE[TB:]:
                if use[0] in ("max", "shift"):
                    top_use(use, cnt)
                else:
                    side(use, 0, cnt)
                if use[0] == "var":
                    coefficients(0)
                    for i in range(PIECES):
                        silu(0, i)
            step(0, 0, cnt, first=True)
            step(0, 1, cnt, first=True)
            with dve.Fori(0, B - 2) as b:
                now = cnt.later(b)
                step(b, 2, now)
                step(b, 3, now)
                step(b + 1, 0, now)
                step(b + 1, 1, now)
            now = cnt.later(B - 2)
            step(B - 2, 2, now)
            step(B - 2, 3, now)
            for s in range(4):
                step(B - 1, s, now, last=True)
            sums(B - 1, 15)
            for use in EPILOGUE:
                side(use, B - 1, now)

        @block.tensor
        def _(pe):
            PASSES = [(c, i, j) for c in range(CC) for i, j in ((0, 0), (0, 1), (1, 0))]

            def three_passes(stationary, moving, part):
                for c, i, j in PASSES if part is None else PASSES[:6] if part == 0 else PASSES[6:]:
                    ins = nc.tensor.matmul(SD[:], stationary(i, c), moving(j, c),
                                           start=(c == 0 and i + j == 0), stop=(c == CC - 1 and i == 1))
                return ins

            def top_use(use, cnt):
                bank = cnt.top_bank
                wait(pe, top_drained, cnt.top - 1)
                if use[0] == "max":
                    _, pair, hh, qb, kh = use
                    r = rows_of(hh)
                    if qb == kh == 0:
                        wait(pe, side_drained, cnt.mark["qk"])
                    ins = nc.tensor.matmul(TP[:, bank], QK_hi[r, pair % 2, 0, bass.ts(qb, P)],
                                           QK_hi[r, pair % 2, 1, bass.ts(kh, HALF)],
                                           start=True, stop=True)
                else:
                    _, pair, hh, half = use
                    pe.wait_ge(shift_ready, cnt.shifts + 1)
                    for i in range(4):
                        qb = 4 * half + i
                        ins = nc.tensor.matmul(TP[:, bank, bass.ts(i, P)], ms[:, hh, qb:qb + 1].to_broadcast([P, P]),
                                               ident16[:], start=True, stop=True)
                ins.then_inc(top_filled, 1)
                cnt.passed(use)

            def side(use, image, cnt, part=None):
                kind = use[0]
                if part != 1:
                    wait(pe, side_drained, cnt.side)
                if kind in ("qk", "v") and part != 1:
                    half = use[3] if kind == "qk" else use[1] // 4
                    pe.wait_ge(xn_lo, PIECES * image + CC * (half + 1))
                if kind == "qk":
                    _, pair, which, half = use
                    col = pair * P + (0 if which == "q" else CH)
                    ins = three_passes(lambda i, c: wq[:, i, c, col:col + P],
                                       lambda j, c: xn[:, j, c, bass.ts(half, HALF)], part)
                if kind == "v":
                    ins = three_passes(lambda i, c: xn[:, i, c, bass.ts(use[1], P)],
                                       lambda j, c: wq[:, j, c, 2 * CH:3 * CH], part)
                if kind == "out":
                    if part != 1:
                        pe.wait_ge(side_drained, cnt.mark["ot"])
                    ins = three_passes(lambda i, c: OT[:, i, c, bass.ts(use[1], P)],
                                       lambda j, c: wo[:, j, c, :], part)
                if part == 0:
                    return
                if kind == "ot":
                    _, pair, half = use
                    pe.wait_ge(o_normed, 16 * image + 4 * (pair + 1))
                    for i in range(4):
                        ins = nc.tensor.transpose(SD[:, bass.ts(i, P)], O32[:, pair % 2, 4 * half + i, :],
                                                  ident32[:])
                if kind == "xt":
                    t = use[1]
                    pe.wait_ge(x_loaded[t % 2], 16 * (TB // 2 * image + t // 2 + 1))
                    for c in range(CC):
                        ins = nc.tensor.transpose(SD[:, bass.ts(c, P)], x_in[:, t % 2, bass.ts(c, P)],
                                                  ident32[:])
                if kind == "mean":
                    pe.wait_ge(chan_stats, image + 1)
                    ins = nc.tensor.matmul(SD[:, 0:CC], group_mean[:], mv[:, :, 0], start=True, stop=True)
                if kind == "var":
                    pe.wait_ge(dev_ready, image + 1)
                    ins = nc.tensor.matmul(SD[:, 0:CC], group_mean[:], vd, start=True, stop=True)
                ins.then_inc(side_filled, 1)
                cnt.passed(use)

            def scores(b, v, i, cnt):
                head, q, kp = v // 8, v // 4 % 2, v % 4
                slot = head_slot(head // 2, head % 2)
                if i == 0:
                    if v % 4 == 0:
                        pe.wait_ge(top_drained, cnt.top - TOPS_SINCE_SHIFT[q])
                    if v % 8 == 0:
                        pe.wait_ge(placed[head % 2], PLACED * (4 * b + head // 2 + 1))
                    wait(pe, exp_done, UNITS * b + v - 1)
                kb = bass.ts(2 * kp + i, P)
                dst = ST[:, v % 2, bass.ts(i, HALF)]
                nc.tensor.matmul(dst, K1[:, slot, kb], Q1[:, slot, bass.ts(q, HALF)], start=True, stop=False)
                ins = nc.tensor.matmul(dst, K2[:, slot, kb], Q2[:, slot, bass.ts(q, HALF)], start=False,
                                       stop=True)
                if i == 1:
                    ins.then_inc(scores_ready, 1)

            def times_v(b, v, i, cnt):
                head, kp = v // 8, v % 4
                if i == 0:
                    pe.wait_ge(exp_done, UNITS * b + v + 1)
                    if v % 2 == 0:
                        pe.wait_ge(lo_dve, 32 * b + v // 2 + 1)
                    else:
                        pe.wait_ge(lo_pool, 32 * b + v // 2 + 1)
                    if kp == 0:
                        wait(pe, pv_out, 16 * b + v // 4)
                    if v == 0:
                        pe.wait_ge(side_drained, cnt.mark["v"])
                    if v == 32:
                        pe.wait_ge(v_moved, b + 1)
                kb = 2 * kp + i
                for qb in range(4):
                    at, to = i * HALF + qb * P, qb * (LO + HD)
                    v_all = V[:, kb, v_slot(head), :]
                    probs_hi, probs_lo = Ph[:, v % 4, at:at + P], Pl[:, v % 4, at:at + P]
                    products = [(slice(to, to + LO + HD), probs_hi, v_all[:, 0:LO + HD])]
                    if qb == 3:
                        products = [(slice(to, to + LO), probs_hi, v_all[:, 0:LO]),
                                    (slice(to, to + HD), probs_hi, v_all[:, LO:LO + HD])]
                    products.append((slice(to, to + LO), probs_lo, v_all[:, 0:LO]))
                    for n, (cols, stationary, moving) in enumerate(products):
                        ins = nc.tensor.matmul(PV[:, cols], stationary, moving, start=kb == qb == n == 0,
                                               stop=kb == TB - 1, skip_group_check=True)
                if i == 1:
                    ins.then_inc(pv_done, 1)

            def step(b, s, cnt, first=False, last=False):
                for u in range(16):
                    v = 16 * s + u
                    sides, tops = side_uses(s, u, first, last), top_uses(s, u, last)
                    before = (b, v - 2) if v >= 2 else (b - 1, UNITS + v - 2)
                    scores(b, v, 0, cnt)
                    scores(b, v, 1, cnt)
                    late = follows_split(s, u, first, last)
                    place = TOP_PLACES[u % 8 == 7][late]
                    for use in tops[:place[0]]:
                        top_use(use, cnt)
                    if not (first and v < 2):
                        times_v(*before, 0, cnt)
                        times_v(*before, 1, cnt)
                    for use in tops[place[0]:place[1]]:
                        top_use(use, cnt)
                    for use in sides:
                        if use[0] in SPLIT:
                            side(use, image_of(use, b, s), cnt, part=0)
                    for use in tops[place[1]:place[2]]:
                        top_use(use, cnt)
                    for use in sides:
                        side(use, image_of(use, b, s), cnt, part=1 if use[0] in SPLIT else None)
                    for use in tops[place[2]:]:
                        top_use(use, cnt)

            cnt = Count()
            pe.wait_ge(const_ready, 5)
            for use in PROLOGUE[:TB]:
                side(use, 0, cnt)
            pe.wait_ge(w_abs_ready, 1)
            for i in range(3):
                for c in range(CC):
                    last_mm = nc.tensor.matmul(bound_psum[:, i, :], bound16[:, c:c + 1].to_broadcast([P, P]),
                                               w_abs[:, c, i * CH:(i + 1) * CH], start=(c == 0),
                                               stop=(c == CC - 1))
            last_mm.then_inc(bound_out, 1)
            pe.wait_ge(setup_done, 1)
            for use in PROLOGUE[TB:]:
                if use[0] in ("max", "shift"):
                    top_use(use, cnt)
                else:
                    side(use, 0, cnt)
            step(0, 0, cnt, first=True)
            step(0, 1, cnt, first=True)
            with pe.Fori(0, B - 2) as b:
                now = cnt.later(b)
                step(b, 2, now)
                step(b, 3, now)
                step(b + 1, 0, now)
                step(b + 1, 1, now)
            now = cnt.later(B - 2)
            step(B - 2, 2, now)
            step(B - 2, 3, now)
            for s in range(4):
                step(B - 1, s, now, last=True)
            for v in (UNITS - 2, UNITS - 1):
                times_v(B - 1, v, 0, now)
                times_v(B - 1, v, 1, now)
            for use in EPILOGUE:
                side(use, B - 1, now)


_INS = ["x", "L0_conv_gn_scale", "L0_conv_gn_offset", "L0_conv_w_qkv", "L0_conv_w_out", "L0_conv_b_out"]


def kernel(**inputs):
    import concourse.bacc as bacc
    from concourse.bass_utils import run_bass_kernel_spmd as run

    nc = bacc.Bacc("TRN2", target_bir_lowering=False, num_devices=1)
    arrays, args = {}, []
    for name in _INS:
        a = np.ascontiguousarray(inputs[name])
        arrays[f"in_{name}"] = a
        args.append(nc.dram_tensor(f"in_{name}", a.shape, mybir.dt.from_np(a.dtype), kind="ExternalInput").ap())
    args.append(nc.dram_tensor("out_0", (B, 32, 32, CH), F32, kind="ExternalOutput").ap())
    conv_attention(nc, *args)
    return run(nc, [arrays], core_ids=[0]).results[0]["out_0"]
```
